# Optimizing a Trainium2 kernel written in Bass

```python
import numpy as np
import jax
import jax.numpy as jnp

def _softmax(x, axis=-1):
    return jax.nn.softmax(x, axis=axis)

def _gelu(x):
    return jax.nn.gelu(x, approximate=True)

def _silu(x):
    return jax.nn.silu(x)

def _sigmoid(x):
    return jax.nn.sigmoid(x)

def _layernorm(x, axis=-1, eps=1e-05):
    m = jnp.mean(x, axis=axis, keepdims=True)
    v = jnp.var(x, axis=axis, keepdims=True)
    return (x - m) / jnp.sqrt(v + eps)

def _scatter_add(tgt, idx, src, axis=0):
    return tgt.at[idx].add(src)

def _segment_sum(src, seg, n):
    return jax.ops.segment_sum(src, seg, n)
kernel_name = 'mk_seq_postln_d1_jaxref_r4_52b46f'

def setup_inputs(seed: int=0):
    np.random.seed(seed)
    _w = jnp.asarray

    def _L0_attn_setup():
        import jax, jax.numpy as jnp
        import numpy as np
        D_MODEL = 256
        N_HEADS = 16
        N_GROUPS = 4
        D_HEAD = D_MODEL // N_HEADS
        HPG = N_HEADS // N_GROUPS
        B, T = (2, 512)

        def _rope(x):
            t, d = (x.shape[2], x.shape[3])
            pos = jnp.arange(t, dtype=jnp.float32)[:, None]
            freq = jnp.exp(-(jnp.arange(0, d, 2, dtype=jnp.float32) / d) * jnp.log(jnp.float32(10000.0)))
            angle = pos * freq
            cos, sin = (jnp.cos(angle), jnp.sin(angle))
            xe, xo = (x[..., ::2], x[..., 1::2])
            re = xe * cos - xo * sin
            ro = xe * sin + xo * cos
            return jnp.stack([re, ro], axis=-1).reshape(x.shape)
        key = jax.random.key(seed)
        ks = jax.random.split(key, 10)
        s = 0.02
        return {'x': jax.random.normal(ks[0], (B, T, D_MODEL), dtype=jnp.float32), 'Wq': jax.random.normal(ks[1], (D_MODEL, D_MODEL), dtype=jnp.float32) * s, 'bq': jax.random.normal(ks[2], (D_MODEL,), dtype=jnp.float32) * s, 'Wk': jax.random.normal(ks[3], (D_MODEL, N_GROUPS * D_HEAD), dtype=jnp.float32) * s, 'bk': jax.random.normal(ks[4], (N_GROUPS * D_HEAD,), dtype=jnp.float32) * s, 'Wv': jax.random.normal(ks[5], (D_MODEL, N_GROUPS * D_HEAD), dtype=jnp.float32) * s, 'bv': jax.random.normal(ks[6], (N_GROUPS * D_HEAD,), dtype=jnp.float32) * s, 'Wo': jax.random.normal(ks[7], (D_MODEL, D_MODEL), dtype=jnp.float32) * s, 'bo': jax.random.normal(ks[8], (D_MODEL,), dtype=jnp.float32) * s}
    _L0_attn_in = _L0_attn_setup()

    def _L0_ffn_setup():
        import jax, jax.numpy as jnp
        import numpy as np
        HIDDEN = 256
        MOE_INTER = 128
        SHARED_INTER = 512
        N_EXPERTS = 32
        TOP_K = 6
        N_GROUP = 8
        TOPK_GROUP = 4
        ROUTED_SCALE = 2.5

        def _relu2(x):
            return jnp.square(jax.nn.relu(x))

        def _router(x, gate_w, e_bias):
            T = x.shape[0]
            logits = x.astype(jnp.float32) @ gate_w.astype(jnp.float32).T
            scores = jax.nn.sigmoid(logits)
            sc = scores + e_bias[None, :]
            g = sc.reshape(T, N_GROUP, N_EXPERTS // N_GROUP)
            group_scores = jax.lax.top_k(g, 2)[0].sum(-1)
            group_idx = jax.lax.top_k(group_scores, TOPK_GROUP)[1]
            group_mask = jnp.zeros_like(group_scores).at[jnp.arange(T)[:, None], group_idx].set(1.0)
            score_mask = jnp.repeat(group_mask, N_EXPERTS // N_GROUP, axis=1)
            masked = jnp.where(score_mask > 0, sc, 0.0)
            topk_idx = jax.lax.stop_gradient(jax.lax.top_k(masked, TOP_K)[1])
            topk_w = jnp.take_along_axis(scores, topk_idx, axis=1)
            topk_w = topk_w / (topk_w.sum(-1, keepdims=True) + 1e-20)
            topk_w = topk_w * ROUTED_SCALE
            return (topk_idx, topk_w)
        if __name__ == '__main__':
            out = reference(**setup_inputs())
            print(out.shape, out.dtype)
        key = jax.random.key(seed)
        ks = jax.random.split(key, 6)
        s = 0.02
        return {'hidden_states': jax.random.normal(ks[0], (2, 256, HIDDEN), jnp.float32), 'gate_w': jax.random.normal(ks[1], (N_EXPERTS, HIDDEN), jnp.float32) * s, 'e_bias': jnp.zeros((N_EXPERTS,), jnp.float32), 'up_w': jax.random.normal(ks[2], (N_EXPERTS, MOE_INTER, HIDDEN), jnp.float32) * s, 'down_w': jax.random.normal(ks[3], (N_EXPERTS, HIDDEN, MOE_INTER), jnp.float32) * s, 'shared_up_w': jax.random.normal(ks[4], (SHARED_INTER, HIDDEN), jnp.float32) * s, 'shared_down_w': jax.random.normal(ks[5], (HIDDEN, SHARED_INTER), jnp.float32) * s}
    _L0_ffn_in = _L0_ffn_setup()
    _d = {'L0_attn_x': _L0_attn_in['x'], 'L0_attn_Wq': _L0_attn_in['Wq'], 'L0_attn_bq': _L0_attn_in['bq'], 'L0_attn_Wk': _L0_attn_in['Wk'], 'L0_attn_bk': _L0_attn_in['bk'], 'L0_attn_Wv': _L0_attn_in['Wv'], 'L0_attn_bv': _L0_attn_in['bv'], 'L0_attn_Wo': _L0_attn_in['Wo'], 'L0_attn_bo': _L0_attn_in['bo'], 'L0_ffn_gate_w': _L0_ffn_in['gate_w'], 'L0_ffn_e_bias': _L0_ffn_in['e_bias'], 'L0_ffn_up_w': _L0_ffn_in['up_w'], 'L0_ffn_down_w': _L0_ffn_in['down_w'], 'L0_ffn_shared_up_w': _L0_ffn_in['shared_up_w'], 'L0_ffn_shared_down_w': _L0_ffn_in['shared_down_w']}
    _x0 = _d['L0_attn_x']
    _d['L0_attn_x'] = jax.random.normal(jax.random.fold_in(jax.random.key(seed), 1), (4, 2048, 256), dtype=_x0.dtype)
    del _x0
    return _d

def reference(L0_attn_x, L0_attn_Wq, L0_attn_bq, L0_attn_Wk, L0_attn_bk, L0_attn_Wv, L0_attn_bv, L0_attn_Wo, L0_attn_bo, L0_ffn_gate_w, L0_ffn_e_bias, L0_ffn_up_w, L0_ffn_down_w, L0_ffn_shared_up_w, L0_ffn_shared_down_w):

    def _L0_attn_ref(x, Wq, bq, Wk, bk, Wv, bv, Wo, bo):
        import jax, jax.numpy as jnp
        import numpy as np
        D_MODEL = 256
        N_HEADS = 16
        N_GROUPS = 4
        D_HEAD = D_MODEL // N_HEADS
        HPG = N_HEADS // N_GROUPS
        B, T = (2, 512)

        def _rope(x):
            t, d = (x.shape[2], x.shape[3])
            pos = jnp.arange(t, dtype=jnp.float32)[:, None]
            freq = jnp.exp(-(jnp.arange(0, d, 2, dtype=jnp.float32) / d) * jnp.log(jnp.float32(10000.0)))
            angle = pos * freq
            cos, sin = (jnp.cos(angle), jnp.sin(angle))
            xe, xo = (x[..., ::2], x[..., 1::2])
            re = xe * cos - xo * sin
            ro = xe * sin + xo * cos
            return jnp.stack([re, ro], axis=-1).reshape(x.shape)
        b, t, _ = x.shape
        q = (x @ Wq + bq).reshape(b, t, N_HEADS, D_HEAD).transpose(0, 2, 1, 3)
        k = (x @ Wk + bk).reshape(b, t, N_GROUPS, D_HEAD).transpose(0, 2, 1, 3)
        v = (x @ Wv + bv).reshape(b, t, N_GROUPS, D_HEAD).transpose(0, 2, 1, 3)
        k = jnp.repeat(k, HPG, axis=1)
        v = jnp.repeat(v, HPG, axis=1)
        q = _rope(q)
        k = _rope(k)
        scale = jnp.float32(np.sqrt(D_HEAD))
        scores = jnp.einsum('bhtd,bhsd->bhts', q, k) / scale
        causal = jnp.tril(jnp.ones((t, t), dtype=bool))
        scores = jnp.where(causal, scores, -jnp.inf)
        probs = jax.nn.softmax(scores, axis=-1)
        attn = jnp.einsum('bhts,bhsd->bhtd', probs, v)
        out = attn.transpose(0, 2, 1, 3).reshape(b, t, N_HEADS * D_HEAD)
        return out @ Wo + bo

    def _L0_ffn_ref(hidden_states, gate_w, e_bias, up_w, down_w, shared_up_w, shared_down_w):
        import jax, jax.numpy as jnp
        import numpy as np
        HIDDEN = 256
        MOE_INTER = 128
        SHARED_INTER = 512
        N_EXPERTS = 32
        TOP_K = 6
        N_GROUP = 8
        TOPK_GROUP = 4
        ROUTED_SCALE = 2.5

        def _relu2(x):
            return jnp.square(jax.nn.relu(x))

        def _router(x, gate_w, e_bias):
            T = x.shape[0]
            logits = x.astype(jnp.float32) @ gate_w.astype(jnp.float32).T
            scores = jax.nn.sigmoid(logits)
            sc = scores + e_bias[None, :]
            g = sc.reshape(T, N_GROUP, N_EXPERTS // N_GROUP)
            group_scores = jax.lax.top_k(g, 2)[0].sum(-1)
            group_idx = jax.lax.top_k(group_scores, TOPK_GROUP)[1]
            group_mask = jnp.zeros_like(group_scores).at[jnp.arange(T)[:, None], group_idx].set(1.0)
            score_mask = jnp.repeat(group_mask, N_EXPERTS // N_GROUP, axis=1)
            masked = jnp.where(score_mask > 0, sc, 0.0)
            topk_idx = jax.lax.stop_gradient(jax.lax.top_k(masked, TOP_K)[1])
            topk_w = jnp.take_along_axis(scores, topk_idx, axis=1)
            topk_w = topk_w / (topk_w.sum(-1, keepdims=True) + 1e-20)
            topk_w = topk_w * ROUTED_SCALE
            return (topk_idx, topk_w)
        if __name__ == '__main__':
            out = reference(**setup_inputs())
            print(out.shape, out.dtype)
        B, S, H = hidden_states.shape
        x = hidden_states.reshape(-1, H)
        T = x.shape[0]
        topk_idx, topk_w = _router(x, gate_w, e_bias)
        combine = jnp.zeros((T, N_EXPERTS), topk_w.dtype).at[jnp.arange(T)[:, None], topk_idx].add(topk_w)
        h = _relu2(jnp.einsum('th,eih->tei', x, up_w))
        h = h * combine[:, :, None]
        moe_out = jnp.einsum('tei,ehi->th', h, down_w)
        shared = _relu2(x @ shared_up_w.T) @ shared_down_w.T
        return (moe_out + shared).reshape(B, S, H)
    x = L0_attn_x
    x = _layernorm(x + _L0_attn_ref(x, L0_attn_Wq, L0_attn_bq, L0_attn_Wk, L0_attn_bk, L0_attn_Wv, L0_attn_bv, L0_attn_Wo, L0_attn_bo), axis=-1)
    x = _layernorm(x + _L0_ffn_ref(x, L0_ffn_gate_w, L0_ffn_e_bias, L0_ffn_up_w, L0_ffn_down_w, L0_ffn_shared_up_w, L0_ffn_shared_down_w), axis=-1)
    return x

_drawn_inputs = setup_inputs


def setup_inputs(seed=0):
    import zlib

    import numpy as np

    out = dict(_drawn_inputs(seed))
    spreads = {'L0_ffn_e_bias': (0.0, 0.28)}
    factors = {'L0_attn_Wq': 8.0,
     'L0_attn_bq': 8.0,
     'L0_attn_Wk': 8.0,
     'L0_attn_bk': 8.0,
     'L0_attn_Wv': 8.0,
     'L0_attn_bv': 7.697,
     'L0_attn_Wo': 5.643,
     'L0_attn_bo': 10.194,
     'L0_ffn_gate_w': 2.989}
    for name, (base, spread) in spreads.items():
        noise = np.random.default_rng([zlib.crc32(name.encode()), seed]).standard_normal(out[name].shape)
        drawn = base * np.exp(spread * noise) if base else spread * noise
        out[name] = jnp.asarray(drawn.astype(out[name].dtype))
    for name, factor in factors.items():
        out[name] = (out[name] * factor).astype(out[name].dtype)
    return out
```

```python
import numpy as np
import concourse.bass as bass
from concourse import mybir
from concourse.alu_op_type import AluOpType as ALU
from contextlib import ExitStack

B, T, D = 4, 2048, 256
NH, NG, DH = 16, 4, 16
HPG = NH // NG
NE, FI, NSH = 32, 128, 512
NX = NE + NSH // FI
NGR, EPG, TOPG, TOPK = 8, 4, 4, 6
EPS = 1e-5
P = 128
C = D // P
NT = T // P
CH = 512
TPC = CH // P
NC = T // CH
QKV = D + 2 * NG * DH
QK = D + NG * DH
ROW = 64
M_ROW = 3 * DH
M_ONE = 64.0
W_UP, W_DN, W_GATE, H_SCALE = 64.0, 64.0, 16.0, 16.0
BIG = 3.0e38


def layer(nc, x, xt, wqkv, bqkv, wo, bo, gate, ebias, up, down, rope_cos, rope_sin,
          eye32, eye16, eyeb, future, select, out):
    f32, f16, bf16 = mybir.dt.float32, mybir.dt.float16, mybir.dt.bfloat16
    ACT = mybir.ActivationFunctionType
    AX = mybir.AxisListType

    ctx = ExitStack()
    with ctx:
        def sb(name, shape, dt, where=ctx):
            return where.enter_context(nc.sbuf_tensor(name, shape, dt))

        def pb(name, shape, dt, where):
            return where.enter_context(nc.psum_tensor(name, shape, dt))

        def sems(where, *names):
            return [where.enter_context(nc.semaphore(n)) for n in names]

        up_w = sb("up_w", [P, NX, C, 2, FI], f16)
        dn_w = sb("dn_w", [P, NX, 2 * D], f16)
        qkv_w = sb("qkv_w", [P, C, 2, QKV], f16)
        wo_w = sb("wo_w", [P, C, 2 * D], f16)
        gate_w = sb("gate_w", [P, C, 2, NE], f16)
        cos_t = sb("cos_t", [P, NT, DH], f32)
        sin_t = sb("sin_t", [P, NT, DH], f32)
        b_qkv = sb("b_qkv", [P, QKV], f32)
        b_o = sb("b_o", [P, D], f32)
        b_e = sb("b_e", [P, NE], f32)
        id32 = sb("id32", [P, P], f32)
        id16 = sb("id16", [P, P], f16)
        idb = sb("idb", [P, P], bf16)
        fut = sb("fut", [P, P], bf16)
        attn = sb("attn", [P, NT * D], f32)
        xhl = attn[:, :].bitcast(f16).rearrange("p (s c t) -> p s c t", s=2, c=C)

        def retire(names):
            numbers = [s.num for s in names]
            assert numbers == list(range(numbers[0], numbers[0] + len(numbers)))
            nc.all_engine_barrier(sems_to_clear=range(numbers[0], numbers[0] + len(numbers)))

        st = ExitStack()
        with st:
            w_stage = sb("w_stage", [P, 2 * NX * C * FI], f32, st)
            s_stage = sb("s_stage", [P, C * (QKV + D + NE)], f32, st)
            n_up = NX * C * FI
            qo, oo, go = 0, C * QKV, C * (QKV + D)
            s_const, s_wup, s_wdn, s_small, s_whi, s_wlo = S = sems(
                st, "s_const", "s_wup", "s_wdn", "s_small", "s_whi", "s_wlo")
            consts = [(cos_t[:, :, :], rope_cos), (sin_t[:, :, :], rope_sin), (b_qkv[:, :], bqkv), (b_o[:, :], bo),
                      (b_e[:, :], ebias), (id32[:, :], eye32), (id16[:, :], eye16), (idb[:, :], eyeb),
                      (fut[:, :], future)]
            splits = [
                (s_small, w_v(s_stage[:, qo:oo], QKV), 1.0, qkv_w[:, :, 0, :], qkv_w[:, :, 1, :]),
                (s_small, w_v(s_stage[:, oo:go], D), 1.0, wo_w[:, :, 0:D], wo_w[:, :, D:2 * D]),
                (s_small, w_v(s_stage[:, go:go + C * NE], NE), W_GATE, gate_w[:, :, 0, :], gate_w[:, :, 1, :]),
                (s_wup, w_stage[:, 0:n_up].rearrange("p (e i) -> p e i", i=FI), W_UP,
                 up_w[:, :, :, 0, :].rearrange("p e c i -> p (e c) i"), up_w[:, :, :, 1, :].rearrange("p e c i -> p (e c) i")),
                (s_wdn, w_stage[:, n_up:2 * n_up].rearrange("p (e i) -> p e i", i=D), W_DN,
                 dn_w[:, :, 0:D], dn_w[:, :, D:2 * D]),
            ]
            block = st.enter_context(nc.Block())

            @block.sync
            def _(sp):
                sp.dma_start(s_stage[:, qo:oo], wqkv).then_inc(s_small, 16)
                sp.dma_start(s_stage[:, oo:go], wo).then_inc(s_small, 16)
                sp.dma_start(s_stage[:, go:go + C * NE], gate).then_inc(s_small, 16)
                sp.dma_start(w_stage[:, 0:n_up], up).then_inc(s_wup, 16)
                sp.dma_start(w_stage[:, n_up:2 * n_up], down).then_inc(s_wdn, 16)
                for dst, src in consts:
                    sp.dma_start(dst, src).then_inc(s_const, 16)
                sp.wait_ge(s_const, 16 * len(consts))

            @block.scalar
            def _(act):
                for s, src, scale, hi, _lo in splits:
                    act.wait_ge(s, 48 if s is s_small else 16)
                    nc.scalar.activation(hi, src, ACT.Copy, scale=scale).then_inc(s_whi, 1)

            @block.vector
            def _(dve):
                for n, (s, src, scale, hi, lo) in enumerate(splits):
                    dve.wait_ge(s_whi, n + 1)
                    nc.vector.scalar_tensor_tensor(out=lo, in0=src, scalar=scale, in1=hi,
                                                   op0=ALU.mult, op1=ALU.subtract).then_inc(s_wlo, 1)
                dve.wait_ge(s_wlo, len(splits))
            del block
            nblk = S
        retire(nblk)

        with nc.Fori(0, B) as b:
            qkv_ctx = ExitStack()
            with qkv_ctx:
                qs = sb("qs", [P, (NH // 2) * T], f16, qkv_ctx)
                ks = sb("ks", [P, 2 * NG * T], f16, qkv_ctx)
                vs = sb("vs", [P, NT, NG * 32], f32, qkv_ctx)
                project(nc, sb, pb, sems, retire, b, xt, xhl, qkv_w, b_qkv, cos_t, sin_t, id16, qs, ks, vs)
                with nc.Fori(0, NG) as g:
                    attend(nc, sb, pb, sems, retire, g, qs, ks, vs, attn, id32, id16, idb, fut)
            ffn_ctx = ExitStack()
            with ffn_ctx:
                x1 = sb("x1", [P, NT * D], f32, ffn_ctx)
                x1t = sb("x1t", [P, 2, C, T], f16, ffn_ctx)
                ct = sb("ct", [P, T], f16, ffn_ctx)
                sel_w = sb("sel_w", [P, NX, P], f16, ffn_ctx)
                route(nc, sb, pb, sems, retire, b, x, select, sel_w, attn, wo_w, b_o, gate_w, b_e, id32, id16, x1, x1t, ct)
                with nc.Fori(0, NC) as n:
                    experts(nc, sb, pb, sems, retire, b, n, up_w, dn_w, sel_w, x1, x1t, ct, out)


def w_v(ap, width):
    return ap.rearrange("p (c n) -> p c n", n=width)


def project(nc, sb, pb, sems, retire, b, xt, xhl, qkv_w, b_qkv, cos_t, sin_t, id16, qs, ks, vs):
    f32, f16 = mybir.dt.float32, mybir.dt.float16
    ACT = mybir.ActivationFunctionType
    ph = ExitStack()
    with ph:
        xs = [sb(f"xs{n}", [P, C, CH], f32, ph) for n in range(2)]
        qkv = [sb(f"qkv{n}", [P, QKV], f32, ph) for n in range(2)]
        rc = [sb(f"rc{n}", [P, QK], f32, ph) for n in range(2)]
        rs = [sb(f"rs{n}", [P, QK], f32, ph) for n in range(2)]
        rot = [sb(f"rot{n}", [P, QK], f32, ph) for n in range(2)]
        qt = [sb(f"qt{n}", [P, NH * ROW], f16, ph) for n in range(2)]
        kt = [sb(f"kt{n}", [P, NG * 2 * P], f16, ph) for n in range(2)]
        pj = [pb(f"pj{n}", [P, 512], f32, ph) for n in range(2)]
        tq = [pb(f"tq{n}", [P, 1024], f16, ph) for n in range(2)]
        tk = [pb(f"tk{n}", [P, 1024], f16, ph) for n in range(2)]
        (s_x0, s_x1, s_xhi, s_xlo, s_proj, s_qkv, s_rc, s_rs, s_rot, s_hi, s_v, s_lo, s_tr, s_tqe, s_tke, s_one, s_set) = S = sems(
            ph, "p_x0", "p_x1", "p_xhi", "p_xlo", "p_proj", "p_qkv", "p_rc", "p_rs", "p_rot", "p_hi", "p_v", "p_lo",
            "p_tr", "p_tqe", "p_tke", "p_one", "p_set")
        s_x = [s_x0, s_x1]
        qsv = qs[:, :].rearrange("p (j t) -> p j t", t=T)
        ksv = ks[:, :].rearrange("p (j t) -> p j t", t=T)
        vsv = vs[:, :, :].rearrange("p i (g c) -> p i g c", c=32)

        def heads(ap):
            return ap.rearrange("p (h d) -> p h d", d=DH)

        def q_rows(n):
            return qt[n][:, :].rearrange("p (h r) -> p h r", r=ROW)

        def k_rows(n, par, at):
            return kt[n][:, :].rearrange("p (g c) -> p g c", g=NG)[:, :, par * (P + ROW) + at:par * (P + ROW) + at + DH]

        ph2 = ExitStack()
        with ph2:
            block = ph2.enter_context(nc.Block())

            @block.sync
            def _(sp):
                for c in range(NC):
                    if c >= 2:
                        sp.wait_ge(s_xlo, c - 1)
                    sp.dma_start(xs[c % 2][:, :, :], xt[bass.ds(b, 1), :, :, c * CH:(c + 1) * CH].rearrange("o p c t -> p (o c) t")
                                 ).then_inc(s_x[c % 2], 16)

            @block.tensor
            def _(pe):
                for s in range(NT + 2):
                    if s < NT:
                        i = s
                        pe.wait_ge(s_xlo, i // TPC + 1)
                        if i >= 2:
                            pe.wait_ge(s_qkv, i - 1)
                        n = 0
                        for c in range(C):
                            for xp, wp in ((0, 0), (0, 1), (1, 0)):
                                mm = nc.tensor.matmul(pj[i % 2][:, 0:QKV], xhl[:, xp, c, i * P:(i + 1) * P], qkv_w[:, c, wp, :],
                                                      start=(n == 0), stop=(n == 3 * C - 1))
                                n += 1
                        mm.then_inc(s_proj, 1)
                    if s >= 2:
                        i = s - 2
                        pe.wait_ge(s_lo, 2 * i + 2 * 1)
                        if i >= 2:
                            pe.wait_ge(s_tqe, i - 1)
                            pe.wait_ge(s_tke, i - 1)
                        for j in range(8):
                            nc.tensor.transpose(tq[i % 2][:, j * P:(j + 1) * P], qt[i % 2][:, j * P:(j + 1) * P], id16[:, :])
                        for j in range(8):
                            mm = nc.tensor.transpose(tk[i % 2][:, j * P:(j + 1) * P], kt[i % 2][:, j * P:(j + 1) * P], id16[:, :])
                        mm.then_inc(s_tr, 1)

            @block.gpsimd
            def _(pool):
                for n in range(2):
                    nc.gpsimd.memset(qt[n][:, :].bitcast(f32), 0.0)
                    nc.gpsimd.memset(kt[n][:, :].bitcast(f32), 0.0).then_inc(s_set, 1)
                pool.wait_ge(s_set, 2)
                for n in range(2):
                    for par in range(2):
                        at = par * (P + ROW) + M_ROW
                        ones = kt[n][:, :].rearrange("p (g c) -> p g c", g=NG)[:, :, at:at + 2]
                        nc.gpsimd.memset(ones, M_ONE).then_inc(s_set, 1)
                nc.gpsimd.memset(vsv[:, :, :, DH:32], 1.0).then_inc(s_one, 1)
                for i in range(NT):
                    pool.wait_ge(s_qkv, i + 1)
                    if i >= 2:
                        pool.wait_ge(s_rot, i - 1)
                    for o in range(2):
                        src = qkv[i % 2][:, 0:QK].rearrange("p (h d e) -> p h d e", e=2, d=DH // 2)[:, :, :, 1 - o]
                        dst = rs[i % 2][:, :].rearrange("p (h d e) -> p h d e", e=2, d=DH // 2)[:, :, :, o]
                        sn = sin_t[:, i:i + 1, :].rearrange("p o (d e) -> p o d e", e=2)[:, :, :, o].to_broadcast([P, NH + NG, DH // 2])
                        nc.gpsimd.tensor_tensor(dst, src, sn, ALU.mult).then_inc(s_rs, 1)

            @block.scalar
            def _(act):
                def split(c):
                    act.wait_ge(s_x[c % 2], 16 * (c // 2 + 1))
                    nc.scalar.activation(xhl[:, 0, :, c * CH:(c + 1) * CH], xs[c % 2][:, :, :], ACT.Copy).then_inc(s_xhi, 1)

                split(0)
                act.wait_ge(s_set, 6)
                for s in range(1, NT + 4):
                    if s % TPC == 2 and s // TPC + 1 < NC:
                        split(s // TPC + 1)
                    if s - 1 < NT:
                        i = s - 1
                        act.wait_ge(s_qkv, i + 1)
                        nc.scalar.activation(vsv[:, i, :, 0:DH], heads(qkv[i % 2][:, QK:QKV]), ACT.Copy).then_inc(s_v, 1)
                        act.wait_ge(s_rot, i + 1)
                        if i >= 2:
                            act.wait_ge(s_tr, i - 1)
                        qh = heads(rot[i % 2][:, 0:D])
                        kh = heads(rot[i % 2][:, D:QK])
                        nc.scalar.activation(q_rows(i % 2)[:, :, 0:DH], qh, ACT.Copy).then_inc(s_hi, 1)
                        nc.scalar.activation(q_rows(i % 2)[:, :, DH:2 * DH], qh, ACT.Copy).then_inc(s_hi, 1)
                        for par in range(2):
                            nc.scalar.activation(k_rows(i % 2, par, 0), kh, ACT.Copy).then_inc(s_hi, 1)
                            nc.scalar.activation(k_rows(i % 2, par, 2 * DH), kh, ACT.Copy).then_inc(s_hi, 1)
                    if s >= 4:
                        i = s - 4
                        act.wait_ge(s_tr, i + 1)
                        nc.scalar.activation(ksv[:, :, i * P:(i + 1) * P], tk[i % 2][:, :].rearrange("p (j t) -> p j t", t=P),
                                             ACT.Copy).then_inc(s_tke, 1)

            @block.vector
            def _(dve):
                def split(c):
                    dve.wait_ge(s_xhi, c + 1)
                    nc.vector.tensor_tensor(xhl[:, 1, :, c * CH:(c + 1) * CH], xs[c % 2][:, :, :],
                                            xhl[:, 0, :, c * CH:(c + 1) * CH], ALU.subtract).then_inc(s_xlo, 1)

                split(0)
                for s in range(NT + 4):
                    if s % TPC == 2 and s // TPC + 1 < NC:
                        split(s // TPC + 1)
                    if s < NT:
                        i = s
                        dve.wait_ge(s_proj, i + 1)
                        if i >= 2:
                            dve.wait_ge(s_v, i - 1)
                            dve.wait_ge(s_rs, 2 * (i - 1))
                        nc.vector.tensor_tensor(qkv[i % 2][:, :], pj[i % 2][:, 0:QKV], b_qkv[:, :], ALU.add).then_inc(s_qkv, 1)
                        dve.wait_ge(s_qkv, i + 1)
                        if i >= 2:
                            dve.wait_ge(s_rot, i - 1)
                        cs = cos_t[:, i:i + 1, :].to_broadcast([P, NH + NG, DH])
                        nc.vector.tensor_tensor(heads(rc[i % 2][:, :]), heads(qkv[i % 2][:, 0:QK]), cs, ALU.mult).then_inc(s_rc, 1)
                    if 1 <= s <= NT:
                        i = s - 1
                        dve.wait_ge(s_rs, 2 * (i + 1))
                        dve.wait_ge(s_rc, i + 1)
                        if i >= 2:
                            dve.wait_ge(s_hi, 6 * (i - 1))
                            dve.wait_ge(s_lo, 2 * (i - 1))
                        nc.vector.tensor_tensor(rot[i % 2][:, :], rc[i % 2][:, :], rs[i % 2][:, :], ALU.add).then_inc(s_rot, 1)
                    if 2 <= s < NT + 2:
                        i = s - 2
                        dve.wait_ge(s_hi, 6 * (i + 1))
                        nc.vector.tensor_tensor(q_rows(i % 2)[:, :, 2 * DH:3 * DH], heads(rot[i % 2][:, 0:D]),
                                                q_rows(i % 2)[:, :, 0:DH], ALU.subtract).then_inc(s_lo, 1)
                        kr = kt[i % 2][:, :].rearrange("p (g c) -> p g c", g=NG)
                        klo = bass.AP(kr.tensor, kr.offset + DH, [kr.ap[0], [2 * P, NG], [P + ROW, 2], [1, DH]])
                        khi = bass.AP(kr.tensor, kr.offset, [kr.ap[0], [2 * P, NG], [P + ROW, 2], [1, DH]])
                        kh = rot[i % 2][:, D:QK].rearrange("p (g o d) -> p g o d", g=NG, o=1).to_broadcast([P, NG, 2, DH])
                        nc.vector.tensor_tensor(klo, kh, khi, ALU.subtract).then_inc(s_lo, 1)
                    if s >= 4 - 1:
                        i = s - 3
                        if i < NT:
                            dve.wait_ge(s_tr, i + 1)
                            nc.vector.tensor_copy(qsv[:, :, i * P:(i + 1) * P],
                                                  tq[i % 2][:, :].rearrange("p (j t) -> p j t", t=P)).then_inc(s_tqe, 1)
        retire(S)


def attend(nc, sb, pb, sems, retire, g, qs, ks, vs, attn, id32, id16, idb, fut):
    f32, f16 = mybir.dt.float32, mybir.dt.float16
    ACT = mybir.ActivationFunctionType
    AX = mybir.AxisListType
    NP = 3

    units, blocks = [], []
    for J in range(NC):
        u = []
        for tt in range(TPC):
            width = (J * TPC + tt + 1) * P
            pieces = [(0, min(width, 1024))] + ([(1024, width - 1024)] if width > 1024 else [])
            for h in range(HPG):
                for n, (c0, w) in enumerate(pieces):
                    u.append((tt, h, n, c0, w, n == len(pieces) - 1))
        units.append(u)
        blocks.append(TPC * (J + 1))
    def share(J, j):
        if J + 1 >= NC:
            return []
        steps = max(1, blocks[J] - 2)
        u = units[J + 1]
        return u[len(u) * min(j, steps) // steps:len(u) * min(j + 1, steps) // steps]

    ph = ExitStack()
    with ph:
        pt = [sb(f"pt{n}", [P, HPG, CH], f32, ph) for n in range(NP)]
        vg = sb("vg", [P, NT, 32], f32, ph)
        mxp = [sb(f"mxp{n}", [P, 2, TPC * HPG], f32, ph) for n in range(2)]
        mrow = [sb(f"mrow{n}", [P, TPC * HPG, 2], f16, ph) for n in range(2)]
        mt = [sb(f"mt{n}", [2 * HPG, CH], f16, ph) for n in range(2)]
        ot = [sb(f"ot{n}", [P, CH], f32, ph) for n in range(2)]
        rec = [sb(f"rec{n}", [P, TPC, HPG], f32, ph) for n in range(2)]
        mx = [pb(f"mx{n}", [P, 1024], f32, ph) for n in range(2)]
        sc = [pb(f"sc{n}", [P, CH], f32, ph) for n in range(2)]
        pv = pb("pv", [P, CH], f32, ph)
        misc = pb("misc", [P, 1024], f16, ph)
        misc32 = misc[:, :].bitcast(f32)
        (s_mx, s_red, s_mrow, s_comb, s_mhi, s_mt, s_mte, s_m, s_sc, s_ex, s_msk, s_pv, s_oe, s_otr, s_on, s_rec, s_vg) = S = sems(
            ph, "a_mx", "a_red", "a_mrow", "a_comb", "a_mhi", "a_mt", "a_mte", "a_m", "a_sc", "a_ex", "a_msk", "a_pv",
            "a_oe", "a_otr", "a_on", "a_rec", "a_vg")
        n_two = [0, 0, 1, 2]
        at = attn[:, :].rearrange("p (i c) -> p i c", c=D)

        ph2 = ExitStack()
        with ph2:
            block = ph2.enter_context(nc.Block())

            @block.sync
            def _(sp):
                for J in range(NC):
                    sp.wait_ge(s_mte, J + 1)
                    for par in range(2):
                        for q in range(2):
                            r = (par * 2 + q) * 2
                            sp.dma_start(qs[ROW * par + M_ROW:ROW * par + M_ROW + 2, bass.ds(g * (2 * T) + q * T + J * CH, CH)],
                                         mt[J % 2][r:r + 2, :]).then_inc(s_m, 16)
                sp.wait_ge(s_m, 64 * NC)

            @block.tensor
            def _(pe):
                n_mx, u_sc, n_pv, n_diag = [0], [0], [0], [0]

                def maximum(J, unit):
                    tt, h, _n, c0, w, last = unit
                    k = n_mx[0]
                    if k >= 2:
                        pe.wait_ge(s_red, k - 1)
                    lhsT = qs[:, bass.ds(g * (2 * T) + (h // 2) * T + (J * TPC + tt) * P, P)]
                    for c in range(0, w, CH):
                        cw = min(CH, w - c)
                        diag = last and c + cw == w
                        mm = nc.tensor.matmul(mx[k % 2][:, c:c + cw], lhsT,
                                              ks[:, bass.ds(g * (2 * T) + (h % 2) * T + c0 + c, cw)], start=True, stop=not diag)
                        if diag:
                            mm = nc.tensor.matmul(mx[k % 2][:, w - P:w], idb[:, :], fut[:, :], start=False, stop=True)
                    mm.then_inc(s_mx, 1)
                    n_mx[0] += 1

                def maximum_rows(J):
                    pe.wait_ge(s_mrow, J + 1)
                    if J >= 1:
                        pe.wait_ge(s_mte, J)
                    if J >= 2:
                        pe.wait_ge(s_on, J - 1)
                    for tt in range(TPC):
                        mm = nc.tensor.transpose(misc[0:2 * HPG, tt * P:(tt + 1) * P],
                                                 mrow[J % 2][:, tt * HPG:(tt + 1) * HPG, :].rearrange("p a b -> p (a b)"), id16[:, :])
                    mm.then_inc(s_mt, 1)

                def scores(J, j, h):
                    r = max(0, j - TPC * J) * P
                    u = u_sc[0]
                    if u >= 2:
                        pe.wait_ge(s_ex, u - 1)
                    nc.tensor.matmul(sc[u % 2][:, 0:CH - r], ks[:, bass.ds(g * (2 * T) + (h % 2) * T + j * P, P)],
                                     qs[:, bass.ds(g * (2 * T) + (h // 2) * T + J * CH + r, CH - r)],
                                     start=True, stop=True).then_inc(s_sc, 1)
                    u_sc[0] += 1

                def values(J, j):
                    k = n_pv[0]
                    r = max(0, j - TPC * J) * P
                    if j >= TPC * J:
                        n_diag[0] += 1
                        pe.wait_ge(s_msk, n_diag[0])
                    else:
                        pe.wait_ge(s_ex, 4 * (k + 1))
                    if j == 0 and J >= 1:
                        pe.wait_ge(s_oe, J)
                    for h in range(HPG):
                        mm = nc.tensor.matmul(pv[32 * h:32 * h + 32, r:CH], vg[:, j, :], pt[k % NP][:, h, r:CH],
                                              start=(j == 0), stop=(j == blocks[J] - 1), tile_position=(0, 32 * h))
                    mm.then_inc(s_pv, 1)
                    n_pv[0] += 1

                def outputs(J):
                    pe.wait_ge(s_oe, J + 1)
                    pe.wait_ge(s_mte, min(J + 2, NC))
                    if J >= 1:
                        pe.wait_ge(s_on, J)
                    for tt in range(TPC):
                        mm = nc.tensor.transpose(misc32[:, tt * P:(tt + 1) * P], ot[J % 2][:, tt * P:(tt + 1) * P], id32[:, :])
                    mm.then_inc(s_otr, 1)

                for unit in units[0]:
                    maximum(0, unit)
                maximum_rows(0)
                pe.wait_ge(s_vg, 1)
                before = None
                for J in range(NC):
                    pe.wait_ge(s_m, 64 * (J + 1))
                    for j in range(blocks[J]):
                        scores(J, j, 0)
                        scores(J, j, 1)
                        if before is not None:
                            values(*before)
                        before = (J, j)
                        scores(J, j, 2)
                        scores(J, j, 3)
                        for unit in share(J, j):
                            maximum(J + 1, unit)
                        if j == blocks[J] - 2 and J + 1 < NC:
                            maximum_rows(J + 1)
                        if j == 1 and J >= 1:
                            outputs(J - 1)
                values(*before)
                outputs(NC - 1)

            @block.scalar
            def _(act):
                k = 0

                def rows_out(J):
                    act.wait_ge(s_mt, J + 1)
                    if J >= 2:
                        act.wait_ge(s_m, 64 * (J - 1))
                    nc.scalar.activation(mt[J % 2][:, :], misc[0:2 * HPG, 0:CH], ACT.Copy).then_inc(s_mte, 1)

                def output_out(J, k):
                    act.wait_ge(s_pv, k)
                    if J >= 2:
                        act.wait_ge(s_otr, J - 1)
                    nc.scalar.activation(ot[J % 2][:, :], pv[:, :], ACT.Copy).then_inc(s_oe, 1)

                rows_out(0)
                for J in range(NC):
                    for j in range(blocks[J]):
                        r = max(0, j - TPC * J) * P
                        if k >= NP:
                            act.wait_ge(s_pv, k - NP + 1)
                        for h in range(HPG):
                            u = 4 * k + h
                            act.wait_ge(s_sc, u + 1)
                            nc.scalar.activation(pt[k % NP][:, h, r:CH], sc[u % 2][:, 0:CH - r], ACT.Exp,
                                                 scale=DH ** -0.5).then_inc(s_ex, 1)
                            if h == 1 and j == 0 and J >= 1:
                                output_out(J - 1, k)
                        k += 1
                        if j == blocks[J] - 2 and J + 1 < NC:
                            rows_out(J + 1)
                output_out(NC - 1, k)

            @block.gpsimd
            def _(pool):
                vv = vs[:, :, :]
                nc.gpsimd.tensor_copy(vg[:, :, :], vs[:, :, bass.ds(g * 32, 32)]).then_inc(s_vg, 1)
                k = 0
                for J in range(NC):
                    for j in range(blocks[J]):
                        if j >= TPC * J:
                            r = (j - TPC * J) * P
                            pool.wait_ge(s_ex, 4 * (k + 1))
                            dg = pt[k % NP][:, :, r:r + P]
                            nc.gpsimd.affine_select(out=dg, in_=dg, compare_op=ALU.is_ge, fill=0.0, base=0,
                                                    pattern=[[0, HPG], [1, P]], channel_multiplier=-1).then_inc(s_msk, 1)
                        k += 1

            @block.vector
            def _(dve):
                n_red = [0]

                def reduce(J, unit):
                    tt, h, n, _c0, w, _last = unit
                    k = n_red[0]
                    dve.wait_ge(s_mx, k + 1)
                    if J >= 2:
                        dve.wait_ge(s_mrow, J - 1)
                    col = tt * HPG + (h % 2) * 2 + h // 2
                    nc.vector.reduce_max(mxp[J % 2][:, n, col:col + 1], mx[k % 2][:, 0:w], AX.X).then_inc(s_red, 1)
                    n_red[0] += 1

                def rows(J):
                    dve.wait_ge(s_red, n_red[0])
                    m = mxp[J % 2][:, 0, :]
                    if len(units[J]) > TPC * HPG:
                        c = len(units[J]) // HPG - TPC
                        a = (TPC - c) * HPG
                        nc.vector.tensor_tensor(mxp[J % 2][:, 0, a:], mxp[J % 2][:, 0, a:], mxp[J % 2][:, 1, a:],
                                                ALU.max).then_inc(s_comb, 1)
                        dve.wait_ge(s_comb, n_two[J])
                    if J >= 2:
                        dve.wait_ge(s_mt, J - 1)
                    nc.vector.tensor_scalar(mrow[J % 2][:, :, 0], m, -1.0 / M_ONE, None, ALU.mult).then_inc(s_mhi, 1)
                    dve.wait_ge(s_mhi, J + 1)
                    nc.vector.scalar_tensor_tensor(out=mrow[J % 2][:, :, 1], in0=m, scalar=-1.0 / M_ONE, in1=mrow[J % 2][:, :, 0],
                                                   op0=ALU.mult, op1=ALU.subtract).then_inc(s_mrow, 1)

                def divide(J):
                    dve.wait_ge(s_otr, J + 1)
                    if J >= 2:
                        dve.wait_ge(s_on, J - 1)
                    o = misc32.rearrange("p (t h c) -> p t h c", h=HPG, c=32)
                    nc.vector.reciprocal(rec[J % 2][:, :, :], o[:, :, :, DH]).then_inc(s_rec, 1)
                    dve.wait_ge(s_rec, J + 1)
                    dst = at[:, J * TPC:(J + 1) * TPC, bass.ds(g * (HPG * DH), HPG * DH)].rearrange("p t (h d) -> p t h d", d=DH)
                    nc.vector.tensor_tensor(dst, o[:, :, :, 0:DH],
                                            rec[J % 2][:, :, :].rearrange("p t (h o) -> p t h o", o=1).to_broadcast([P, TPC, HPG, DH]),
                                            ALU.mult).then_inc(s_on, 1)

                for unit in units[0]:
                    reduce(0, unit)
                rows(0)
                for J in range(NC):
                    for j in range(blocks[J]):
                        for unit in share(J, j):
                            reduce(J + 1, unit)
                        if j == blocks[J] - 2 and J + 1 < NC:
                            rows(J + 1)
                        if j == 1 and J >= 1:
                            divide(J - 1)
                divide(NC - 1)
        retire(S)


def norm_steps(nc, dve, y, st, mv, sd, rstd, s_st, s_mv, s_sd, s_rs, n):
    nc.vector.bn_stats(st, y).then_inc(s_st, 1)
    dve.wait_ge(s_st, n + 1)
    nc.vector.bn_aggr(mv, st).then_inc(s_mv, 1)
    dve.wait_ge(s_sd, n + 1)
    nc.vector.reciprocal(rstd, sd).then_inc(s_rs, 1)
    dve.wait_ge(s_rs, n + 1)


def route(nc, sb, pb, sems, retire, b, x, select, sel_w, attn, wo_w, b_o, gate_w, b_e, id32, id16, x1, x1t, ct):
    f32, f16 = mybir.dt.float32, mybir.dt.float16
    ACT = mybir.ActivationFunctionType
    AX = mybir.AxisListType
    ph = ExitStack()
    with ph:
        xin = sb("xin", [P, NT, D], f32, ph)
        ah = [sb(f"ah{n}", [P, D], f16, ph) for n in range(2)]
        al = [sb(f"al{n}", [P, D], f16, ph) for n in range(2)]
        y0 = [sb(f"y0{n}", [P, D], f32, ph) for n in range(2)]
        y1 = [sb(f"y1{n}", [P, D], f32, ph) for n in range(2)]
        st = [sb(f"st{n}", [P, 6], f32, ph) for n in range(2)]
        mv = [sb(f"mv{n}", [P, 2], f32, ph) for n in range(2)]
        eps = sb("eps", [P, 1], f32, ph)
        sd = [sb(f"sd{n}", [P, 1], f32, ph) for n in range(2)]
        rstd = [sb(f"rstd{n}", [P, 1], f32, ph) for n in range(2)]
        score = sb("score", [P, NT, NE], f32, ph)
        bsc = sb("bsc", [P, NT, NE], f32, ph)
        pmax = sb("pmax", [P, NT, NGR, 2], f32, ph)
        psum2 = sb("psum2", [P, NT, NGR, 2], f32, ph)
        gsc = sb("gsc", [P, NT, NGR], f32, ph)
        gs2 = sb("gs2", [P, NT, NGR], f32, ph)
        gtop = sb("gtop", [P, NT, 8], f32, ph)
        grep = sb("grep", [P, NT, NGR], f32, ph)
        gsel = sb("gsel", [P, NT, NGR], f32, ph)
        masked = sb("masked", [P, NT, NE], f32, ph)
        etop = sb("etop", [P, NT, 8], f32, ph)
        erep = sb("erep", [P, NT, NE], f32, ph)
        wgt = sb("wgt", [P, NT, NE], f32, ph)
        wsum = sb("wsum", [P, NT], f32, ph)
        cst = sb("cst", [P, NT, P], f16, ph)
        ap_ = [pb(f"ap{n}", [P, CH], f32, ph) for n in range(2)]
        wp_ = [pb(f"wp{n}", [P, CH], f32, ph) for n in range(2)]
        xp_ = [pb(f"xp{n}", [P, CH], f32, ph) for n in range(2)]
        lg = pb("lg", [P, CH], f32, ph)
        cp = pb("cp", [P, 1024], f16, ph)
        (s_x, s_xb, s_at, s_ah, s_al, s_w, s_y0, s_y1, s_st, s_mv, s_sd, s_eps, s_rs, s_n, s_xt, s_xh, s_xl, s_lg, s_sig, s_r, s_c0, s_ct, s_cte, s_sel) = S = sems(
            ph, "r_x", "r_xb", "r_at", "r_ah", "r_al", "r_w", "r_y0", "r_y1", "r_st", "r_mv", "r_sd", "r_epsd", "r_rs", "r_n", "r_xt", "r_xh",
            "r_xl", "r_lg", "r_sig", "r_r", "r_c0", "r_ct", "r_cte", "r_sel")
        x1v = x1[:, :].rearrange("p (i c) -> p i c", c=D)

        ph2 = ExitStack()
        with ph2:
            block = ph2.enter_context(nc.Block())

            @block.sync
            def _(sp):
                sp.dma_start(xin[:, :, :], x[bass.ds(b, 1), :, :].rearrange("o (i p) c -> p (o i) c", p=P)).then_inc(s_x, 16)
                sp.dma_start(sel_w[:, :, :], select).then_inc(s_sel, 16)
                sp.wait_ge(s_sel, 16)

            @block.gpsimd
            def _(pool):
                nc.gpsimd.memset(eps[:, :], EPS).then_inc(s_eps, 1)
                nc.gpsimd.memset(cst[:, :, :], 0.0).then_inc(s_c0, 1)
                pool.wait_ge(s_c0, 1)
                nc.gpsimd.memset(cst[:, :, NE:NX], 1.0).then_inc(s_c0, 1)
                pool.wait_ge(s_x, 16)
                for i in range(NT):
                    nc.gpsimd.tensor_tensor(x1v[:, i, :], xin[:, i, :], b_o[:, :], ALU.add).then_inc(s_xb, 1)

            @block.tensor
            def _(pe):
                for s in range(NT + 4):
                    if s < NT:
                        i = s
                        if i >= 2:
                            pe.wait_ge(s_al, i - 1)
                        for c in range(C):
                            mm = nc.tensor.transpose(ap_[i % 2][:, c * P:(c + 1) * P], attn[:, i * D + c * P:i * D + (c + 1) * P], id32[:, :])
                        mm.then_inc(s_at, 1)
                    if 1 <= s <= NT:
                        i = s - 1
                        pe.wait_ge(s_al, i + 1)
                        if i >= 2:
                            pe.wait_ge(s_y1, i - 1)
                        for c in range(C):
                            nc.tensor.matmul(wp_[i % 2][:, :], ah[i % 2][:, c * P:(c + 1) * P], wo_w[:, c, :], start=(c == 0), stop=False)
                        for c in range(C):
                            mm = nc.tensor.matmul(wp_[i % 2][:, 0:D], al[i % 2][:, c * P:(c + 1) * P], wo_w[:, c, 0:D],
                                                  start=False, stop=(c == C - 1))
                        mm.then_inc(s_w, 1)
                    if 3 <= s < NT + 3:
                        i = s - 3
                        pe.wait_ge(s_n, i + 1)
                        if i >= 2:
                            pe.wait_ge(s_xl, i - 1)
                        for c in range(C):
                            mm = nc.tensor.transpose(xp_[i % 2][:, c * P:(c + 1) * P], x1[:, i * D + c * P:i * D + (c + 1) * P], id32[:, :])
                        mm.then_inc(s_xt, 1)
                    if s >= 4:
                        i = s - 4
                        pe.wait_ge(s_xl, i + 1)
                        n = 0
                        for c in range(C):
                            for xh, wh in ((0, 0), (0, 1), (1, 0)):
                                mm = nc.tensor.matmul(lg[:, i * NE:(i + 1) * NE], x1t[:, xh, c, i * P:(i + 1) * P], gate_w[:, c, wh, :],
                                                      start=(n == 0), stop=(n == 3 * C - 1))
                                n += 1
                        mm.then_inc(s_lg, 1)
                for half in range(2):
                    pe.wait_ge(s_ct, 2)
                    if half:
                        pe.wait_ge(s_cte, 1)
                    for n in range(8):
                        mm = nc.tensor.transpose(cp[:, n * P:(n + 1) * P], cst[:, half * 8 + n, :], id16[:, :])
                    mm.then_inc(s_lg, 1)

            @block.scalar
            def _(act):
                for s in range(NT + 4):
                    if s < NT:
                        i = s
                        act.wait_ge(s_at, i + 1)
                        if i >= 2:
                            act.wait_ge(s_w, i - 1)
                        nc.scalar.activation(ah[i % 2][:, :], ap_[i % 2][:, 0:D], ACT.Copy).then_inc(s_ah, 1)
                    if 2 <= s < NT + 2:
                        i = s - 2
                        act.wait_ge(s_mv, i + 1)
                        if i == 0:
                            act.wait_ge(s_eps, 1)
                        if i >= 2:
                            act.wait_ge(s_rs, i - 1)
                        nc.scalar.activation(sd[i % 2][:, :], mv[i % 2][:, 1:2], ACT.Sqrt, bias=eps[:, :]).then_inc(s_sd, 1)
                    if 3 <= s < NT + 3:
                        i = s - 3
                        act.wait_ge(s_xt, i + 1)
                        nc.scalar.activation(x1t[:, 0, :, i * P:(i + 1) * P], xp_[i % 2][:, 0:D].rearrange("p (c t) -> p c t", c=C),
                                             ACT.Copy).then_inc(s_xh, 1)
                act.wait_ge(s_lg, NT)
                nc.scalar.activation(score[:, :, :], lg[:, :].rearrange("p (i e) -> p i e", e=NE), ACT.Sigmoid,
                                     scale=1.0 / W_GATE).then_inc(s_sig, 1)
                for half in range(2):
                    act.wait_ge(s_lg, NT + half + 1)
                    nc.scalar.activation(ct[:, half * 1024:(half + 1) * 1024], cp[:, :], ACT.Copy).then_inc(s_cte, 1)

            @block.vector
            def _(dve):
                for s in range(NT + 4):
                    if s < NT:
                        i = s
                        dve.wait_ge(s_ah, i + 1)
                        if i >= 2:
                            dve.wait_ge(s_w, i - 1)
                        nc.vector.tensor_tensor(al[i % 2][:, :], ap_[i % 2][:, 0:D], ah[i % 2][:, :], ALU.subtract).then_inc(s_al, 1)
                    if 2 <= s < NT + 2:
                        i = s - 2
                        dve.wait_ge(s_w, i + 1)
                        dve.wait_ge(s_xb, i + 1)
                        if i >= 2:
                            dve.wait_ge(s_n, i - 1)
                        nc.vector.tensor_tensor(y0[i % 2][:, :], wp_[i % 2][:, 0:D], x1v[:, i, :], ALU.add).then_inc(s_y0, 1)
                        dve.wait_ge(s_y0, i + 1)
                        nc.vector.tensor_tensor(y1[i % 2][:, :], wp_[i % 2][:, D:2 * D], y0[i % 2][:, :], ALU.add).then_inc(s_y1, 1)
                        dve.wait_ge(s_y1, i + 1)
                        norm_steps(nc, dve, y1[i % 2][:, :], st[i % 2][:, :], mv[i % 2][:, :], sd[i % 2][:, :], rstd[i % 2][:, :], s_st, s_mv, s_sd, s_rs, i)
                        nc.vector.tensor_scalar(x1v[:, i, :], y1[i % 2][:, :], mv[i % 2][:, 0:1], rstd[i % 2][:, :],
                                                ALU.subtract, ALU.mult).then_inc(s_n, 1)
                    if 3 <= s < NT + 3:
                        i = s - 3
                        dve.wait_ge(s_xh, i + 1)
                        nc.vector.tensor_tensor(x1t[:, 1, :, i * P:(i + 1) * P], xp_[i % 2][:, 0:D].rearrange("p (c t) -> p c t", c=C),
                                                x1t[:, 0, :, i * P:(i + 1) * P], ALU.subtract).then_inc(s_xl, 1)

                done = [0]

                def link(op):
                    done[0] += 1
                    op.then_inc(s_r, 1)
                    dve.wait_ge(s_r, done[0])

                V = nc.vector
                dve.wait_ge(s_sig, 1)
                link(V.tensor_tensor(bsc[:, :, :], score[:, :, :], b_e[:, :].rearrange("p (o e) -> p o e", o=1).to_broadcast([P, NT, NE]), ALU.add))
                pr = bsc[:, :, :].rearrange("p i (g a e) -> p (i g) a e", a=2, e=2)
                pm, p2 = (t[:, :, :, :].rearrange("p i g a -> p (i g) a") for t in (pmax, psum2))
                link(V.tensor_tensor(pm, pr[:, :, :, 0], pr[:, :, :, 1], ALU.max))
                link(V.tensor_tensor(p2, pr[:, :, :, 0], pr[:, :, :, 1], ALU.add))
                gv, g2 = (t[:, :, :].rearrange("p i g -> p (i g)") for t in (gsc, gs2))
                link(V.tensor_tensor(gv, pm[:, :, 0], pm[:, :, 1], ALU.add))
                link(V.tensor_tensor(g2, p2[:, :, 0], p2[:, :, 1], ALU.max))
                link(V.tensor_tensor(gv, gv, g2, ALU.max))
                for i in range(NT):
                    op = V.max(gtop[:, i, :], gsc[:, i, :])
                    op.then_inc(s_r, 1)
                done[0] += NT
                dve.wait_ge(s_r, done[0])
                link(V.memset(gtop[:, :, TOPG:8], BIG))
                for i in range(NT):
                    V.match_replace(grep[:, i, :], gtop[:, i, :], gsc[:, i, :], -BIG).then_inc(s_r, 1)
                done[0] += NT
                dve.wait_ge(s_r, done[0])
                link(V.tensor_scalar(gsel[:, :, :], grep[:, :, :], -BIG, None, ALU.is_equal))
                link(V.tensor_tensor(masked[:, :, :].rearrange("p i (g e) -> p (i g) e", e=EPG), bsc[:, :, :].rearrange("p i (g e) -> p (i g) e", e=EPG),
                                     gsel[:, :, :].rearrange("p i (g o) -> p (i g) o", o=1).to_broadcast([P, NT * NGR, EPG]), ALU.mult))
                for i in range(NT):
                    V.max(etop[:, i, :], masked[:, i, :]).then_inc(s_r, 1)
                done[0] += NT
                dve.wait_ge(s_r, done[0])
                link(V.memset(etop[:, :, TOPK:8], BIG))
                for i in range(NT):
                    V.match_replace(erep[:, i, :], etop[:, i, :], masked[:, i, :], -BIG).then_inc(s_r, 1)
                done[0] += NT
                dve.wait_ge(s_r, done[0])
                link(V.scalar_tensor_tensor(out=wgt[:, :, :].rearrange("p i e -> p (i e)"), in0=erep[:, :, :].rearrange("p i e -> p (i e)"), scalar=-BIG,
                                            in1=score[:, :, :].rearrange("p i e -> p (i e)"), op0=ALU.is_equal, op1=ALU.mult))
                link(V.reduce_sum(wsum[:, :], wgt[:, :, :], AX.X))
                link(V.tensor_scalar(wsum[:, :], wsum[:, :], 1e-20, None, ALU.add))
                link(V.reciprocal(wsum[:, :], wsum[:, :]))
                link(V.scalar_tensor_tensor(out=wgt[:, :, :], in0=wgt[:, :, :], scalar=2.5,
                                            in1=wsum[:, :].rearrange("p (i o) -> p i o", o=1).to_broadcast([P, NT, NE]), op0=ALU.mult, op1=ALU.mult))
                dve.wait_ge(s_c0, 2)
                V.tensor_copy(cst[:, :, 0:NE], wgt[:, :, :]).then_inc(s_ct, 1)
                dve.wait_ge(s_ct, 1)
                V.tensor_tensor(cst[:, :, NX:NX + NE], wgt[:, :, :], cst[:, :, 0:NE], ALU.subtract).then_inc(s_ct, 1)
        retire(S)


def experts(nc, sb, pb, sems, retire, b, n, up_w, dn_w, sel_w, x1, x1t, ct, out):
    f32, f16 = mybir.dt.float32, mybir.dt.float16
    ACT = mybir.ActivationFunctionType
    NB = 3
    ph = ExitStack()
    with ph:
        r = [sb(f"e_r{k}", [P, CH], f32, ph) for k in range(NB)]
        r2 = [sb(f"e_r2{k}", [P, CH], f32, ph) for k in range(NB)]
        h = [sb(f"e_h{k}", [P, CH], f32, ph) for k in range(NB)]
        hh = [sb(f"e_hh{k}", [P, CH], f16, ph) for k in range(NB)]
        hl = [sb(f"e_hl{k}", [P, CH], f16, ph) for k in range(NB)]
        t0 = [sb(f"e_t0{k}", [P, D], f32, ph) for k in range(TPC)]
        t1 = [sb(f"e_t1{k}", [P, D], f32, ph) for k in range(2)]
        t2 = [sb(f"e_t2{k}", [P, D], f32, ph) for k in range(2)]
        st = [sb(f"e_st{k}", [P, 6], f32, ph) for k in range(2)]
        mv = [sb(f"e_mv{k}", [P, 2], f32, ph) for k in range(2)]
        eps = sb("e_eps", [P, 1], f32, ph)
        sd = [sb(f"e_sd{k}", [P, 1], f32, ph) for k in range(2)]
        rstd = [sb(f"e_rstd{k}", [P, 1], f32, ph) for k in range(2)]
        yo = sb("e_yo", [P, TPC, D], f32, ph)
        z = [pb(f"e_z{k}", [P, CH], f32, ph) for k in range(2)]
        cb = [pb(f"e_cb{k}", [P, CH], f32, ph) for k in range(2)]
        o = [pb(f"e_o{k}", [P, 2 * D], f32, ph) for k in range(TPC)]
        (s_z, s_r, s_r2, s_cb, s_h, s_hi, s_lo, s_dn, s_t0, s_t1, s_t2, s_st, s_mv, s_sd, s_eps, s_rs, s_n, s_out) = S = sems(
            ph, "e_z", "e_r", "e_r2", "e_cb", "e_h", "e_hi", "e_lo", "e_dn", "e_t0", "e_t1", "e_t2", "e_st", "e_mv", "e_sd", "e_epsd", "e_rs",
            "e_n", "e_out")
        cols = bass.ds(n * CH, CH)
        un = 1.0 / (H_SCALE * W_DN)
        x1v = x1[:, :].rearrange("p (i c) -> p i c", c=D)
        outv = out.rearrange("b (i p) c -> p (b i) c", p=P)

        ph2 = ExitStack()
        with ph2:
            block = ph2.enter_context(nc.Block())

            @block.tensor
            def _(pe):
                for s in range(NX + 2):
                    if s < NX:
                        e = s
                        if e >= 2:
                            pe.wait_ge(s_r, e - 1)
                        k = 0
                        for c in range(C):
                            for xh, wh in ((0, 0), (1, 0), (0, 1)):
                                mm = nc.tensor.matmul(z[e % 2][:, :], up_w[:, e, c, wh, :], x1t[:, xh, c, cols],
                                                      start=(k == 0), stop=(k == 3 * C - 1))
                                k += 1
                        mm.then_inc(s_z, 1)
                        if e >= 2:
                            pe.wait_ge(s_h, e - 1)
                        nc.tensor.matmul(cb[e % 2][:, :], sel_w[:, e, :], ct[:, cols], start=True, stop=True).then_inc(s_cb, 1)
                    if s >= 2:
                        e = s - 2
                        pe.wait_ge(s_lo, e + 1)
                        for k in range(TPC):
                            nc.tensor.matmul(o[k][:, :], hh[e % NB][:, k * P:(k + 1) * P], dn_w[:, e, :], start=(e == 0), stop=False)
                            mm = nc.tensor.matmul(o[k][:, 0:D], hl[e % NB][:, k * P:(k + 1) * P], dn_w[:, e, 0:D],
                                                  start=False, stop=(e == NX - 1))
                        mm.then_inc(s_dn, 1)

            @block.scalar
            def _(act):
                for s in range(NX + 1):
                    if s < NX:
                        e = s
                        act.wait_ge(s_z, e + 1)
                        if e >= NB:
                            act.wait_ge(s_r2, e - NB + 1)
                        nc.scalar.activation(r[e % NB][:, :], z[e % 2][:, :], ACT.Relu, scale=H_SCALE ** 0.5 / W_UP).then_inc(s_r, 1)
                    if s >= 1:
                        e = s - 1
                        act.wait_ge(s_h, e + 1)
                        if e >= NB:
                            act.wait_ge(s_dn, e - NB + 1)
                        nc.scalar.activation(hh[e % NB][:, :], h[e % NB][:, :], ACT.Copy).then_inc(s_hi, 1)
                act.wait_ge(s_dn, NX)
                for k in range(TPC):
                    nc.scalar.activation(t0[k][:, :], o[k][:, D:2 * D], ACT.Copy, scale=un).then_inc(s_t0, 1)
                act.wait_ge(s_eps, 1)
                for k in range(TPC):
                    act.wait_ge(s_mv, k + 1)
                    if k >= 2:
                        act.wait_ge(s_rs, k - 1)
                    nc.scalar.activation(sd[k % 2][:, :], mv[k % 2][:, 1:2], ACT.Sqrt, bias=eps[:, :]).then_inc(s_sd, 1)

            @block.gpsimd
            def _(pool):
                nc.gpsimd.memset(eps[:, :], EPS).then_inc(s_eps, 1)
                for e in range(NX):
                    pool.wait_ge(s_r, e + 1)
                    if e >= NB:
                        pool.wait_ge(s_h, e - NB + 1)
                    nc.gpsimd.tensor_tensor(r2[e % NB][:, :], r[e % NB][:, :], r[e % NB][:, :], ALU.mult).then_inc(s_r2, 1)

            @block.vector
            def _(dve):
                for s in range(NX + 1):
                    if s < NX:
                        e = s
                        dve.wait_ge(s_r2, e + 1)
                        dve.wait_ge(s_cb, e + 1)
                        if e >= NB:
                            dve.wait_ge(s_lo, e - NB + 1)
                        nc.vector.tensor_tensor(h[e % NB][:, :], r2[e % NB][:, :], cb[e % 2][:, :], ALU.mult).then_inc(s_h, 1)
                    if s >= 1:
                        e = s - 1
                        dve.wait_ge(s_hi, e + 1)
                        if e >= NB:
                            dve.wait_ge(s_dn, e - NB + 1)
                        nc.vector.tensor_tensor(hl[e % NB][:, :], h[e % NB][:, :], hh[e % NB][:, :], ALU.subtract).then_inc(s_lo, 1)
                for k in range(TPC):
                    dve.wait_ge(s_t0, k + 1)
                    if k >= 2:
                        dve.wait_ge(s_t2, k - 1)
                    nc.vector.scalar_tensor_tensor(out=t1[k % 2][:, :], in0=o[k][:, 0:D], scalar=un, in1=t0[k][:, :],
                                                   op0=ALU.mult, op1=ALU.add).then_inc(s_t1, 1)
                    dve.wait_ge(s_t1, k + 1)
                    if k >= 2:
                        dve.wait_ge(s_n, k - 1)
                    nc.vector.tensor_tensor(t2[k % 2][:, :], t1[k % 2][:, :], x1[:, bass.ds(n * (TPC * D) + k * D, D)], ALU.add).then_inc(s_t2, 1)
                    dve.wait_ge(s_t2, k + 1)
                    norm_steps(nc, dve, t2[k % 2][:, :], st[k % 2][:, :], mv[k % 2][:, :], sd[k % 2][:, :], rstd[k % 2][:, :], s_st, s_mv, s_sd, s_rs, k)
                    nc.vector.tensor_scalar(yo[:, k, :], t2[k % 2][:, :], mv[k % 2][:, 0:1], rstd[k % 2][:, :],
                                            ALU.subtract, ALU.mult).then_inc(s_n, 1)

            @block.sync
            def _(sp):
                for k in range(TPC):
                    sp.wait_ge(s_n, k + 1)
                    sp.dma_start(outv[:, bass.ds(b * NT + n * TPC + k, 1), :], yo[:, k:k + 1, :]).then_inc(s_out, 16)
                sp.wait_ge(s_out, 16 * TPC)
        retire(S)


def kernel(**inputs):
    import ml_dtypes
    import concourse.bacc as _bacc
    from concourse.bass_utils import run_bass_kernel_spmd as _run

    a = {k.removeprefix("L0_"): np.asarray(v) for k, v in inputs.items()}

    def rows(w):
        return w.reshape(C, P, -1).transpose(1, 0, 2)

    def every(v):
        return np.broadcast_to(v.reshape(1, -1), (P, v.size))

    up = np.concatenate([a["ffn_up_w"], a["ffn_shared_up_w"].reshape(NSH // FI, FI, D)])
    down = np.concatenate([a["ffn_down_w"], a["ffn_shared_down_w"].reshape(D, NSH // FI, FI).transpose(1, 0, 2)])
    arrays = {
        "x": a["attn_x"],
        "xt": a["attn_x"].reshape(B, T, C, P).transpose(0, 3, 2, 1),
        "wqkv": rows(np.concatenate([a["attn_Wq"], a["attn_Wk"], a["attn_Wv"]], axis=1)),
        "bqkv": every(np.concatenate([a["attn_bq"], a["attn_bk"], a["attn_bv"]])),
        "wo": rows(a["attn_Wo"]),
        "bo": every(a["attn_bo"]),
        "gate": rows(a["ffn_gate_w"].T),
        "ebias": every(a["ffn_e_bias"]),
        "up": up.reshape(NX, FI, C, P).transpose(3, 0, 2, 1),
        "down": down.transpose(2, 0, 1),
    }
    pos = np.arange(T, dtype=np.float32)[:, None]
    freq = np.exp(-(np.arange(0, DH, 2, dtype=np.float32) / DH) * np.log(np.float32(10000.0)))
    angle = pos * freq
    cos = np.repeat(np.cos(angle), 2, axis=1)
    sin = np.stack([-np.sin(angle), np.sin(angle)], axis=-1).reshape(T, DH)
    tiles = lambda t: t.reshape(NT, P, DH).transpose(1, 0, 2).astype(np.float32)
    select = np.zeros((P, NX, P), np.float16)
    for e in range(NX):
        select[e, e] = select[NX + e, e] = 1.0
    arrays |= {
        "rope_cos": tiles(cos), "rope_sin": tiles(sin),
        "eye32": np.eye(P, dtype=np.float32), "eye16": np.eye(P, dtype=np.float16), "eyeb": np.eye(P, dtype=ml_dtypes.bfloat16),
        "future": np.where(np.arange(P)[None, :] > np.arange(P)[:, None], -1e30, 0.0).astype(ml_dtypes.bfloat16),
        "select": select,
    }
    nc = _bacc.Bacc("TRN2", target_bir_lowering=False, num_devices=1)
    aps = {}
    for name, v in arrays.items():
        arrays[name] = v = np.ascontiguousarray(v)
        aps[name] = nc.dram_tensor(name, v.shape, mybir.dt.from_np(v.dtype), kind="ExternalInput").ap()
    aps["out"] = nc.dram_tensor("out", (B, T, D), mybir.dt.float32, kind="ExternalOutput").ap()
    layer(nc, **aps)
    return _run(nc, [arrays], core_ids=[0]).results[0]["out"]
```

```python
import numpy as np
import concourse.bass as bass
from concourse import mybir
from concourse.alu_op_type import AluOpType as ALU
from contextlib import ExitStack

B, T, D = 4, 2048, 256
NH, NG, DH = 16, 4, 16
HPG = NH // NG
NE, FI, NSH = 32, 128, 512
NX = NE + NSH // FI
NGR, EPG, TOPG, TOPK = 8, 4, 4, 6
EPS = 1e-5
P = 128
C = D // P
NT = T // P
CH = 512
TPC = CH // P
NC = T // CH
QKV = D + 2 * NG * DH
QK = D + NG * DH
ROW = 3 * DH
M_ROW = 2 * ROW
M_ONE = 64.0
W_UP, W_DN, W_GATE, H_SCALE = 64.0, 64.0, 16.0, 16.0
BIG = 3.0e38
FIRST, LIMIT, RATE, OVER = 8, 96, 0.85, 600


def layer(nc, x, xt, wqkv, bqkv, wo, bo, gate, ebias, up, down, rope_cos, rope_sin,
          eye32, eye16, eyeb, future, select, out):
    f32, f16, bf16 = mybir.dt.float32, mybir.dt.float16, mybir.dt.bfloat16
    ACT = mybir.ActivationFunctionType
    AX = mybir.AxisListType

    ctx = ExitStack()
    with ctx:
        def sb(name, shape, dt, where=ctx):
            return where.enter_context(nc.sbuf_tensor(name, shape, dt))

        def pb(name, shape, dt, where):
            return where.enter_context(nc.psum_tensor(name, shape, dt))

        def sems(where, *names):
            return [where.enter_context(nc.semaphore(n)) for n in names]

        up_w = sb("up_w", [P, NX, C, 2, FI], f16)
        dn_w = sb("dn_w", [P, NX, 2 * D], f16)
        qkv_w = sb("qkv_w", [P, C, 2, QKV], f16)
        wo_w = sb("wo_w", [P, C, 2 * D], f16)
        gate_w = sb("gate_w", [P, C, 2, NE], f16)
        b_o = sb("b_o", [P, D], f32)
        b_e = sb("b_e", [P, NE], f32)
        id32 = sb("id32", [P, P], f32)
        id16 = sb("id16", [P, P], f16)
        idb = sb("idb", [P, P], bf16)
        fut = sb("fut", [P, P], bf16)
        attn = sb("attn", [P, NT * D], f32)
        xhl = attn[:, :].bitcast(f16).rearrange("p (s c t) -> p s c t", s=2, c=C)

        def retire(names):
            numbers = [s.num for s in names]
            assert numbers == list(range(numbers[0], numbers[0] + len(numbers)))
            nc.all_engine_barrier(sems_to_clear=range(numbers[0], numbers[0] + len(numbers)))

        st = ExitStack()
        with st:
            w_stage = sb("w_stage", [P, 2 * NX * C * FI], f32, st)
            s_stage = sb("s_stage", [P, C * (QKV + D + NE)], f32, st)
            n_up = NX * C * FI
            qo, oo, go = 0, C * QKV, C * (QKV + D)
            s_const, s_wup, s_wdn, s_small, s_whi, s_wlo = S = sems(
                st, "s_const", "s_wup", "s_wdn", "s_small", "s_whi", "s_wlo")
            consts = [(b_o[:, :], bo),
                      (b_e[:, :], ebias), (id32[:, :], eye32), (id16[:, :], eye16), (idb[:, :], eyeb),
                      (fut[:, :], future)]
            splits = [
                (s_small, w_v(s_stage[:, qo:oo], QKV), 1.0, qkv_w[:, :, 0, :], qkv_w[:, :, 1, :]),
                (s_small, w_v(s_stage[:, oo:go], D), 1.0, wo_w[:, :, 0:D], wo_w[:, :, D:2 * D]),
                (s_small, w_v(s_stage[:, go:go + C * NE], NE), W_GATE, gate_w[:, :, 0, :], gate_w[:, :, 1, :]),
                (s_wup, w_stage[:, 0:n_up].rearrange("p (e i) -> p e i", i=FI), W_UP,
                 up_w[:, :, :, 0, :].rearrange("p e c i -> p (e c) i"), up_w[:, :, :, 1, :].rearrange("p e c i -> p (e c) i")),
                (s_wdn, w_stage[:, n_up:2 * n_up].rearrange("p (e i) -> p e i", i=D), W_DN,
                 dn_w[:, :, 0:D], dn_w[:, :, D:2 * D]),
            ]
            block = st.enter_context(nc.Block())

            @block.sync
            def _(sp):
                sp.dma_start(s_stage[:, qo:oo], wqkv).then_inc(s_small, 16)
                sp.dma_start(s_stage[:, oo:go], wo).then_inc(s_small, 16)
                sp.dma_start(s_stage[:, go:go + C * NE], gate).then_inc(s_small, 16)
                sp.dma_start(w_stage[:, 0:n_up], up).then_inc(s_wup, 16)
                sp.dma_start(w_stage[:, n_up:2 * n_up], down).then_inc(s_wdn, 16)
                for dst, src in consts:
                    sp.dma_start(dst, src).then_inc(s_const, 16)
                sp.wait_ge(s_const, 16 * len(consts))

            @block.scalar
            def _(act):
                for s, src, scale, hi, _lo in splits:
                    act.wait_ge(s, 48 if s is s_small else 16)
                    nc.scalar.activation(hi, src, ACT.Copy, scale=scale).then_inc(s_whi, 1)

            @block.vector
            def _(dve):
                for n, (s, src, scale, hi, lo) in enumerate(splits):
                    dve.wait_ge(s_whi, n + 1)
                    nc.vector.scalar_tensor_tensor(out=lo, in0=src, scalar=scale, in1=hi,
                                                   op0=ALU.mult, op1=ALU.subtract).then_inc(s_wlo, 1)
                dve.wait_ge(s_wlo, len(splits))
            del block
            nblk = S
        retire(nblk)

        with nc.Fori(0, B) as b:
            qkv_ctx = ExitStack()
            with qkv_ctx:
                qs = sb("qs", [P, (NH // 2) * T], f16, qkv_ctx)
                ks = sb("ks", [P, 2 * NG * T], f16, qkv_ctx)
                vs = sb("vs", [P, NT, NG * DH], f32, qkv_ctx)
                project(nc, sb, pb, sems, retire, b, xt, xhl, qkv_w, bqkv, rope_cos, rope_sin, id16, qs, ks, vs)
                attend(nc, sb, pb, sems, retire, qs, ks, vs, attn, id32, id16, idb, fut)
            ffn_ctx = ExitStack()
            with ffn_ctx:
                x1 = sb("x1", [P, NT * D], f32, ffn_ctx)
                x1t = sb("x1t", [P, 2, C, T], f16, ffn_ctx)
                ct = sb("ct", [P, T], f16, ffn_ctx)
                sel_w = sb("sel_w", [P, NX, P], f16, ffn_ctx)
                route(nc, sb, pb, sems, retire, b, x, select, sel_w, attn, wo_w, b_o, gate_w, b_e, id32, id16, x1, x1t, ct)
                experts(nc, sb, pb, sems, retire, b, up_w, dn_w, sel_w, x1, x1t, ct, out)


def w_v(ap, width):
    return ap.rearrange("p (c n) -> p c n", n=width)


def project(nc, sb, pb, sems, retire, b, xt, xhl, qkv_w, bqkv, rope_cos, rope_sin, id16, qs, ks, vs):
    f32, f16 = mybir.dt.float32, mybir.dt.float16
    ACT = mybir.ActivationFunctionType
    NQ = 3
    ph = ExitStack()
    with ph:
        xs = [sb(f"xs{n}", [P, C, CH], f32, ph) for n in range(2)]
        qkv = [sb(f"qkv{n}", [P, QKV], f32, ph) for n in range(2)]
        rc = [sb(f"rc{n}", [P, QK], f32, ph) for n in range(2)]
        rs = [sb(f"rs{n}", [P, QK], f32, ph) for n in range(2)]
        rot = [sb(f"rot{n}", [P, QK], f32, ph) for n in range(2)]
        qt = [sb(f"qt{n}", [P, (NH // 2) * P], f16, ph) for n in range(NQ)]
        kt = [sb(f"kt{n}", [P, NG * 2 * P], f16, ph) for n in range(NQ)]
        cos_t = sb("cos_t", [P, NT, DH], f32, ph)
        sin_t = sb("sin_t", [P, NT, DH], f32, ph)
        b_qkv = sb("b_qkv", [P, QKV], f32, ph)
        pj = [pb(f"pj{n}", [P, 512], f32, ph) for n in range(2)]
        tq = [pb(f"tq{n}", [P, 1024], f16, ph) for n in range(2)]
        tk = [pb(f"tk{n}", [P, 1024], f16, ph) for n in range(2)]
        (s_x0, s_x1, s_xhi, s_xlo, s_proj, s_qkv, s_rc, s_rs, s_rot, s_hi, s_v, s_lo, s_tr, s_tqe, s_tke, s_set, s_tab) = S = sems(
            ph, "p_x0", "p_x1", "p_xhi", "p_xlo", "p_proj", "p_qkv", "p_rc", "p_rs", "p_rot", "p_hi", "p_v", "p_lo",
            "p_tr", "p_tqe", "p_tke", "p_set", "p_tab")
        s_x = [s_x0, s_x1]
        qsv = qs[:, :].rearrange("p (j t) -> p j t", t=T)
        ksv = ks[:, :].rearrange("p (j t) -> p j t", t=T)

        def heads(ap):
            return ap.rearrange("p (h d) -> p h d", d=DH)

        def q_rows(n, at):
            return qt[n][:, :].rearrange("p (j r) -> p j r", r=P)[:, :, 0:2 * ROW].rearrange("p j (e r) -> p j e r", e=2)[:, :, :, at:at + DH]

        def k_rows(n, par, at):
            return kt[n][:, :].rearrange("p (g c) -> p g c", g=NG)[:, :, par * (P + ROW) + at:par * (P + ROW) + at + DH]

        def pairs(ap):
            return ap.rearrange("p (j e d) -> p j e d", e=2, d=DH)

        ph2 = ExitStack()
        with ph2:
            block = ph2.enter_context(nc.Block())

            @block.sync
            def _(sp):
                for dst, src in ((b_qkv[:, :], bqkv), (cos_t[:, :, :], rope_cos), (sin_t[:, :, :], rope_sin)):
                    sp.dma_start(dst, src).then_inc(s_tab, 16)
                for c in range(NC):
                    if c >= 2:
                        sp.wait_ge(s_xlo, c - 1)
                    sp.dma_start(xs[c % 2][:, :, :], xt[bass.ds(b, 1), :, :, c * CH:(c + 1) * CH].rearrange("o p c t -> p (o c) t")
                                 ).then_inc(s_x[c % 2], 16)

            @block.tensor
            def _(pe):
                for s in range(NT + 3):
                    if s < NT:
                        i = s
                        pe.wait_ge(s_xlo, i // TPC + 1)
                        if i >= 2:
                            pe.wait_ge(s_qkv, i - 1)
                        n = 0
                        for c in range(C):
                            for xp, wp in ((0, 0), (0, 1), (1, 0)):
                                mm = nc.tensor.matmul(pj[i % 2][:, 0:QKV], xhl[:, xp, c, i * P:(i + 1) * P], qkv_w[:, c, wp, :],
                                                      start=(n == 0), stop=(n == 3 * C - 1))
                                n += 1
                        mm.then_inc(s_proj, 1)
                    if s >= 3:
                        i = s - 3
                        pe.wait_ge(s_lo, 2 * (i + 1))
                        if i >= 2:
                            pe.wait_ge(s_tqe, i - 1)
                            pe.wait_ge(s_tke, i - 1)
                        for j in range(8):
                            nc.tensor.transpose(tq[i % 2][:, j * P:(j + 1) * P], qt[i % NQ][:, j * P:(j + 1) * P], id16[:, :])
                        for j in range(8):
                            mm = nc.tensor.transpose(tk[i % 2][:, j * P:(j + 1) * P], kt[i % NQ][:, j * P:(j + 1) * P], id16[:, :])
                        mm.then_inc(s_tr, 1)

            @block.gpsimd
            def _(pool):
                for n in range(NQ):
                    nc.gpsimd.memset(qt[n][:, :].bitcast(f32), 0.0).then_inc(s_set, 1)
                    nc.gpsimd.memset(kt[n][:, :].bitcast(f32), 0.0).then_inc(s_set, 1)
                pool.wait_ge(s_set, 2 * NQ)
                for n in range(NQ):
                    for par in range(2):
                        at = par * P + M_ROW + 2 * par
                        ones = kt[n][:, :].rearrange("p (g c) -> p g c", g=NG)[:, :, at:at + 2]
                        nc.gpsimd.memset(ones, M_ONE).then_inc(s_set, 1)
                pool.wait_ge(s_tab, 48)
                for i in range(NT):
                    pool.wait_ge(s_qkv, i + 1)
                    if i >= 2:
                        pool.wait_ge(s_rot, i - 1)
                    for o in range(2):
                        src = qkv[i % 2][:, 0:QK].rearrange("p (h d e) -> p h d e", e=2, d=DH // 2)[:, :, :, 1 - o]
                        dst = rs[i % 2][:, :].rearrange("p (h d e) -> p h d e", e=2, d=DH // 2)[:, :, :, o]
                        sn = sin_t[:, i:i + 1, :].rearrange("p o (d e) -> p o d e", e=2)[:, :, :, o].to_broadcast([P, NH + NG, DH // 2])
                        nc.gpsimd.tensor_tensor(dst, src, sn, ALU.mult).then_inc(s_rs, 1)

            @block.scalar
            def _(act):
                def split(c):
                    act.wait_ge(s_x[c % 2], 16 * (c // 2 + 1))
                    nc.scalar.activation(xhl[:, 0, :, c * CH:(c + 1) * CH], xs[c % 2][:, :, :], ACT.Copy).then_inc(s_xhi, 1)

                split(0)
                split(1)
                act.wait_ge(s_set, 4 * NQ)
                for s in range(1, NT + 4):
                    if s >= 4:
                        i = s - 4
                        act.wait_ge(s_tr, i + 1)
                        nc.scalar.activation(ksv[:, :, i * P:(i + 1) * P], tk[i % 2][:, :].rearrange("p (j t) -> p j t", t=P),
                                             ACT.Copy).then_inc(s_tke, 1)
                    if s - 1 < NT:
                        i = s - 1
                        act.wait_ge(s_qkv, i + 1)
                        nc.scalar.activation(vs[:, i, :], qkv[i % 2][:, QK:QKV], ACT.Copy).then_inc(s_v, 1)
                        act.wait_ge(s_rot, i + 1)
                        if i >= NQ:
                            act.wait_ge(s_tr, i - NQ + 1)
                        qh = pairs(rot[i % 2][:, 0:D])
                        kh = heads(rot[i % 2][:, D:QK])
                        nc.scalar.activation(q_rows(i % NQ, 0), qh, ACT.Copy).then_inc(s_hi, 1)
                        nc.scalar.activation(q_rows(i % NQ, DH), qh, ACT.Copy).then_inc(s_hi, 1)
                        for par in range(2):
                            nc.scalar.activation(k_rows(i % NQ, par, 0), kh, ACT.Copy).then_inc(s_hi, 1)
                            nc.scalar.activation(k_rows(i % NQ, par, 2 * DH), kh, ACT.Copy).then_inc(s_hi, 1)
                    if s % TPC == 1 and s // TPC + 2 < NC:
                        split(s // TPC + 2)

            @block.vector
            def _(dve):
                def split(c):
                    dve.wait_ge(s_xhi, c + 1)
                    nc.vector.tensor_tensor(xhl[:, 1, :, c * CH:(c + 1) * CH], xs[c % 2][:, :, :],
                                            xhl[:, 0, :, c * CH:(c + 1) * CH], ALU.subtract).then_inc(s_xlo, 1)

                split(0)
                dve.wait_ge(s_tab, 48)
                for s in range(NT + 4):
                    if s >= 4:
                        i = s - 4
                        dve.wait_ge(s_tr, i + 1)
                        nc.vector.tensor_copy(qsv[:, :, i * P:(i + 1) * P],
                                              tq[i % 2][:, :].rearrange("p (j t) -> p j t", t=P)).then_inc(s_tqe, 1)
                    if s < NT:
                        i = s
                        dve.wait_ge(s_proj, i + 1)
                        if i >= 2:
                            dve.wait_ge(s_v, i - 1)
                            dve.wait_ge(s_rs, 2 * (i - 1))
                        nc.vector.tensor_tensor(qkv[i % 2][:, :], pj[i % 2][:, 0:QKV], b_qkv[:, :], ALU.add).then_inc(s_qkv, 1)
                    if 2 <= s < NT + 2:
                        i = s - 2
                        dve.wait_ge(s_hi, 6 * (i + 1))
                        nc.vector.tensor_tensor(q_rows(i % NQ, 2 * DH), pairs(rot[i % 2][:, 0:D]), q_rows(i % NQ, 0),
                                                ALU.subtract).then_inc(s_lo, 1)
                        kr = kt[i % NQ][:, :].rearrange("p (g c) -> p g c", g=NG)
                        klo = bass.AP(kr.tensor, kr.offset + DH, [kr.ap[0], [2 * P, NG], [P + ROW, 2], [1, DH]])
                        khi = bass.AP(kr.tensor, kr.offset, [kr.ap[0], [2 * P, NG], [P + ROW, 2], [1, DH]])
                        kh = rot[i % 2][:, D:QK].rearrange("p (g o d) -> p g o d", g=NG, o=1).to_broadcast([P, NG, 2, DH])
                        nc.vector.tensor_tensor(klo, kh, khi, ALU.subtract).then_inc(s_lo, 1)
                    if 1 <= s <= NT:
                        i = s - 1
                        dve.wait_ge(s_rs, 2 * (i + 1))
                        dve.wait_ge(s_rc, i + 1)
                        if i >= 2:
                            dve.wait_ge(s_hi, 6 * (i - 1))
                            dve.wait_ge(s_lo, 2 * (i - 1))
                        nc.vector.tensor_tensor(rot[i % 2][:, :], rc[i % 2][:, :], rs[i % 2][:, :], ALU.add).then_inc(s_rot, 1)
                    if s < NT:
                        i = s
                        dve.wait_ge(s_qkv, i + 1)
                        if i >= 2:
                            dve.wait_ge(s_rot, i - 1)
                        cs = cos_t[:, i:i + 1, :].to_broadcast([P, NH + NG, DH])
                        nc.vector.tensor_tensor(heads(rc[i % 2][:, :]), heads(qkv[i % 2][:, 0:QK]), cs, ALU.mult).then_inc(s_rc, 1)
                    if s % TPC == 1 and s // TPC + 1 < NC:
                        split(s // TPC + 1)
        retire(S)


def attend(nc, sb, pb, sems, retire, qs, ks, vs, attn, id32, id16, idb, fut):
    f32, f16 = mybir.dt.float32, mybir.dt.float16
    ACT = mybir.ActivationFunctionType
    AX = mybir.AxisListType
    NP, NSC, NMX, NV = 4, 3, 3, 2
    SKEW = 2
    ORDER = ((0, 0.2), (1, 0.4), (None, 0.6), (2, 0.8), (3, 1.0))

    QCH = [0, 1, 2, 3] + [0, 3, 1, 2] * 2 + [3, 1, 2, 0]
    units = []
    steps = []
    done = []
    for c in range(NG * NC):
        J = QCH[c]
        for tt in range(TPC):
            width = (J * TPC + tt + 1) * P
            for h in range(HPG):
                for n in range(-(-width // CH)):
                    w = min(CH, width - n * CH)
                    units.append((c, tt, h, n, n * CH, w, n * CH + w == width))
        done.append(len(units))
        steps += [(c, j) for j in range(TPC * (J + 1))]

    starts = [steps.index((c, 0)) for c in range(len(done))]
    def pe_unit(n):
        return units[n][5] / 2.4 + (P / 2.4 if units[n][6] else 0)

    def dve_unit(n):
        return units[n][5] / 0.96 + 65

    plan, n = [], 0
    first = done[0] + FIRST
    over = 0.0
    n = first
    for k, (c, j) in enumerate(steps):
        w = CH - max(0, j - TPC * QCH[c]) * P
        time, reduced, a = HPG * w * (1 + 1.1) / 2.4 + 100, over, n
        due = max([done[x] for x in range(len(done)) if starts[x] - (TPC if x > 1 else 2) <= k + 1])
        while n < len(units) and (n < due or (reduced < RATE * time and n < done[c] + LIMIT)):
            time, reduced, n = time + pe_unit(n), reduced + dve_unit(n), n + 1
        over = max(-OVER, min(OVER, reduced - RATE * time))
        plan.append((list(range(a, n)), [x for x in range(len(done)) if a < done[x] <= n]))
    assert n == len(units)
    first_rows = [c for c in range(len(done)) if done[c] <= first]
    ends = [k for k in range(len(steps)) if k + 1 == len(steps) or steps[k + 1][1] == 0]

    ph = ExitStack()
    with ph:
        pt = [sb(f"pt{n}", [P, HPG, CH], f32, ph) for n in range(NP)]
        vg = [sb(f"vg{n}", [P, NT, 32], f32, ph) for n in range(NV)]
        mxp = [sb(f"mxp{n}", [P, NC, TPC * HPG], f32, ph) for n in range(2)]
        mrow = [sb(f"mrow{n}", [P, TPC * HPG, 2], f16, ph) for n in range(2)]
        mcol = [sb(f"mcol{n}", [P, TPC * HPG], f32, ph) for n in range(2)]
        mt = [sb(f"mt{n}", [2 * HPG, CH], f16, ph) for n in range(2)]
        ot = sb("ot", [P, CH], f32, ph)
        rec = sb("rec", [P, TPC, HPG], f32, ph)
        mx = [pb(f"mx{n}", [P, CH], f32, ph) for n in range(NMX)]
        sc = [pb(f"sc{n}", [P, CH], f32, ph) for n in range(NSC)]
        pv = pb("pv", [P, CH], f32, ph)
        misc = pb("misc", [P, 1024], f16, ph)
        misc32 = misc[:, :].bitcast(f32)
        (s_mx, s_red, s_comb, s_mhi, s_mrow, s_mt, s_mte, s_m0, s_m1, s_sc, s_ex, s_msk, s_pv, s_oe, s_otr, s_on, s_rec, s_vg, s_one) = S = sems(
            ph, "a_mx", "a_red", "a_comb", "a_mhi", "a_mrow", "a_mt", "a_mte", "a_m0", "a_m1", "a_sc", "a_ex", "a_msk", "a_pv",
            "a_oe", "a_otr", "a_on", "a_rec", "a_vg", "a_one")
        s_m = [s_m0, s_m1]
        at = attn[:, :].rearrange("p (i c) -> p i c", c=D)

        def qcol(c, h):
            return (c // NC * 2 + h // 2) * T + QCH[c] * CH

        def kcol(c, h):
            return (c // NC * 2 + h % 2) * T

        def first_query(k):
            c, j = steps[k]
            return max(0, j - TPC * QCH[c]) * P

        def diagonals(k):
            return sum(j >= TPC * QCH[c] for c, j in steps[:k + 1])

        ph2 = ExitStack()
        with ph2:
            block = ph2.enter_context(nc.Block())

            @block.sync
            def _(sp):
                for c in range(len(done)):
                    sp.wait_ge(s_mte, c + 1)
                    for q in range(2):
                        to = qcol(c, 2 * q)
                        sp.dma_start(qs[M_ROW:M_ROW + 4, to:to + CH], mt[c % 2][4 * q:4 * q + 4, :]).then_inc(s_m[c % 2], 16)
                for n in range(2):
                    sp.wait_ge(s_m[n], 16 * len(done))

            @block.tensor
            def _(pe):
                n_rows, n_out = 0, 0

                def maximum(n):
                    c, tt, h, _n, c0, w, last = units[n]
                    if n >= NMX:
                        pe.wait_ge(s_red, n - NMX + 1)
                    out = mx[n % NMX]
                    mm = nc.tensor.matmul(out[:, 0:w], qs[:, qcol(c, h) + tt * P:qcol(c, h) + (tt + 1) * P],
                                          ks[:, kcol(c, h) + c0:kcol(c, h) + c0 + w], start=True, stop=not last)
                    if last:
                        mm = nc.tensor.matmul(out[:, w - P:w], idb[:, :], fut[:, :], start=False, stop=True)
                    mm.then_inc(s_mx, 1)

                def misc_free():
                    if n_rows:
                        pe.wait_ge(s_mte, n_rows)
                    if n_out:
                        pe.wait_ge(s_on, n_out)

                def maximum_rows(c):
                    pe.wait_ge(s_mrow, c + 1)
                    misc_free()
                    for tt in range(TPC):
                        mm = nc.tensor.transpose(misc[0:2 * HPG, tt * P:(tt + 1) * P],
                                                 mrow[c % 2][:, tt * HPG:(tt + 1) * HPG, :].rearrange("p a b -> p (a b)"), id16[:, :])
                    mm.then_inc(s_mt, 1)

                def scores(k, h):
                    c, j = steps[k]
                    r = first_query(k)
                    u = HPG * k + h
                    if u >= NSC:
                        pe.wait_ge(s_ex, u - NSC + 1)
                    nc.tensor.matmul(sc[u % NSC][:, 0:CH - r], ks[:, kcol(c, h) + j * P:kcol(c, h) + (j + 1) * P],
                                     qs[:, qcol(c, h) + r:qcol(c, h) + CH], start=True, stop=True).then_inc(s_sc, 1)

                def values(k):
                    c, j = steps[k]
                    r = first_query(k)
                    if j >= TPC * QCH[c]:
                        pe.wait_ge(s_msk, diagonals(k))
                    else:
                        pe.wait_ge(s_ex, HPG * (k + 1))
                    if j == 0:
                        pe.wait_ge(s_vg, c // NC + 1)
                        if c:
                            pe.wait_ge(s_oe, c)
                    for h in range(HPG):
                        mm = nc.tensor.matmul(pv[32 * h:32 * h + 32, r:CH], vg[c // NC % NV][:, j, :], pt[k % NP][:, h, r:CH],
                                              start=(j == 0), stop=(k in ends), tile_position=(0, 32 * h))
                    mm.then_inc(s_pv, 1)

                def outputs(c):
                    pe.wait_ge(s_oe, c + 1)
                    misc_free()
                    for tt in range(TPC):
                        mm = nc.tensor.transpose(misc32[:, tt * P:(tt + 1) * P], ot[:, tt * P:(tt + 1) * P], id32[:, :])
                    mm.then_inc(s_otr, 1)

                for n in range(first):
                    maximum(n)
                for c in first_rows:
                    maximum_rows(c)
                    n_rows += 1
                rows = []
                for k, (c, j) in enumerate(steps):
                    us = list(plan[k][0])
                    if j == 0:
                        pe.wait_ge(s_m[c % 2], 32 * (c // 2 + 1))
                    for op, share in ORDER:
                        if op is not None:
                            scores(k, op)
                        elif k >= SKEW:
                            values(k - SKEW)
                        while us and (plan[k][0][-1] - len(us) + 1.5 - plan[k][0][0]) / len(plan[k][0]) <= share:
                            maximum(us.pop(0))
                    for x in rows:
                        maximum_rows(x)
                        n_rows += 1
                    rows = plan[k][1]
                    if j == SKEW and c:
                        outputs(c - 1)
                        n_out += 1
                for k in range(len(steps) - SKEW, len(steps)):
                    values(k)
                outputs(len(done) - 1)

            @block.scalar
            def _(act):
                def rows_out(c):
                    act.wait_ge(s_mt, c + 1)
                    if c >= 2:
                        act.wait_ge(s_m[c % 2], 32 * (c // 2))
                    nc.scalar.activation(mt[c % 2][:, :], misc[0:2 * HPG, 0:CH], ACT.Copy).then_inc(s_mte, 1)

                def output_out(c):
                    act.wait_ge(s_pv, ends[c] + 1)
                    if c:
                        act.wait_ge(s_otr, c)
                    nc.scalar.activation(ot[:, :], pv[:, :], ACT.Copy).then_inc(s_oe, 1)

                for c in first_rows:
                    rows_out(c)
                rows = []
                for k, (c, j) in enumerate(steps):
                    r = first_query(k)
                    if k >= NP:
                        act.wait_ge(s_pv, k - NP + 1)
                    for h in range(HPG):
                        u = HPG * k + h
                        act.wait_ge(s_sc, u + 1)
                        nc.scalar.activation(pt[k % NP][:, h, r:CH], sc[u % NSC][:, 0:CH - r], ACT.Exp,
                                             scale=DH ** -0.5).then_inc(s_ex, 1)
                        if h == 1 and j == SKEW - 1 and c:
                            output_out(c - 1)
                    for x in rows:
                        rows_out(x)
                    rows = plan[k][1]
                output_out(len(done) - 1)

            @block.gpsimd
            def _(pool):
                for n in range(NV):
                    nc.gpsimd.memset(vg[n][:, :, DH:32], 1.0).then_inc(s_one, 1)
                for k, (c, j) in enumerate(steps):
                    if j == 0 and c % NC == 0:
                        g = c // NC
                        if g >= NV:
                            pool.wait_ge(s_pv, ends[(g - NV + 1) * NC - 1] + 1)
                        nc.gpsimd.tensor_copy(vg[g % NV][:, :, 0:DH], vs[:, :, g * DH:(g + 1) * DH]).then_inc(s_vg, 1)
                    if j >= TPC * QCH[c]:
                        r = first_query(k)
                        pool.wait_ge(s_ex, HPG * (k + 1))
                        dg = pt[k % NP][:, :, r:r + P]
                        nc.gpsimd.affine_select(out=dg, in_=dg, compare_op=ALU.is_ge, fill=0.0, base=0,
                                                pattern=[[0, HPG], [1, P]], channel_multiplier=-1).then_inc(s_msk, 1)

            @block.vector
            def _(dve):
                def reduce(n):
                    c, tt, h, piece, _c0, w, _last = units[n]
                    dve.wait_ge(s_mx, n + 1)
                    if c >= 2:
                        dve.wait_ge(s_mrow, c - 1)
                    col = tt * HPG + h
                    nc.vector.reduce_max(mxp[c % 2][:, piece, col:col + 1], mx[n % NMX][:, 0:w], AX.X).then_inc(s_red, 1)

                def rows(c):
                    dve.wait_ge(s_red, done[c])
                    if c >= 2:
                        dve.wait_ge(s_mrow, c - 1)
                        dve.wait_ge(s_mt, c - 1)
                    m = mcol[c % 2]
                    nc.vector.reduce_max(m[:, :], mxp[c % 2][:, 0:QCH[c] + 1, :].rearrange("p n c -> p c n"), AX.X).then_inc(s_comb, 1)
                    dve.wait_ge(s_comb, c + 1)
                    nc.vector.tensor_scalar(mrow[c % 2][:, :, 0], m[:, :], -1.0 / M_ONE, None, ALU.mult).then_inc(s_mhi, 1)
                    dve.wait_ge(s_mhi, c + 1)
                    nc.vector.scalar_tensor_tensor(out=mrow[c % 2][:, :, 1], in0=m[:, :], scalar=-1.0 / M_ONE, in1=mrow[c % 2][:, :, 0],
                                                   op0=ALU.mult, op1=ALU.subtract).then_inc(s_mrow, 1)

                def divide(c):
                    g, J = c // NC, QCH[c]
                    dve.wait_ge(s_otr, c + 1)
                    if c:
                        dve.wait_ge(s_on, c)
                    o = misc32.rearrange("p (t h c) -> p t h c", h=HPG, c=32)
                    nc.vector.reciprocal(rec[:, :, :], o[:, :, :, DH]).then_inc(s_rec, 1)
                    dve.wait_ge(s_rec, c + 1)
                    dst = at[:, J * TPC:(J + 1) * TPC, g * HPG * DH:(g + 1) * HPG * DH].rearrange("p t (h d) -> p t h d", d=DH)
                    nc.vector.tensor_tensor(dst, o[:, :, :, 0:DH],
                                            rec[:, :, :].rearrange("p t (h o) -> p t h o", o=1).to_broadcast([P, TPC, HPG, DH]),
                                            ALU.mult).then_inc(s_on, 1)

                for n in range(first):
                    reduce(n)
                for c in first_rows:
                    rows(c)
                for k, (c, j) in enumerate(steps):
                    for n in plan[k][0]:
                        reduce(n)
                    for x in plan[k][1]:
                        rows(x)
                    if j == SKEW and c:
                        divide(c - 1)
                divide(len(done) - 1)
        retire(S)


def route(nc, sb, pb, sems, retire, b, x, select, sel_w, attn, wo_w, b_o, gate_w, b_e, id32, id16, x1, x1t, ct):
    f32, f16 = mybir.dt.float32, mybir.dt.float16
    ACT = mybir.ActivationFunctionType
    AX = mybir.AxisListType
    ph = ExitStack()
    with ph:
        xin = sb("xin", [P, NT, D], f32, ph)
        ah = [sb(f"ah{n}", [P, D], f16, ph) for n in range(3)]
        al = [sb(f"al{n}", [P, D], f16, ph) for n in range(3)]
        st = sb("st", [P, NT, 6], f32, ph)
        mv = sb("mv", [P, NT, 2], f32, ph)
        eps = sb("eps", [P, 1], f32, ph)
        sd = sb("sd", [P, NT], f32, ph)
        rstd = sb("rstd", [P, NT], f32, ph)
        score = sb("score", [P, NT, NE], f32, ph)
        bsc = sb("bsc", [P, NT, NE], f32, ph)
        pmax = sb("pmax", [P, NT, NGR, 2], f32, ph)
        psum2 = sb("psum2", [P, NT, NGR, 2], f32, ph)
        gsc = sb("gsc", [P, NT, NGR], f32, ph)
        gs2 = sb("gs2", [P, NT, NGR], f32, ph)
        gtop = sb("gtop", [P, NT, 8], f32, ph)
        grep = sb("grep", [P, NT, NGR], f32, ph)
        gsel = sb("gsel", [P, NT, NGR], f32, ph)
        masked = sb("masked", [P, NT, NE], f32, ph)
        etop = sb("etop", [P, NT, 8], f32, ph)
        erep = sb("erep", [P, NT, NE], f32, ph)
        wgt = sb("wgt", [P, NT, NE], f32, ph)
        wsum = sb("wsum", [P, NT], f32, ph)
        cst = sb("cst", [P, NT, P], f16, ph)
        ap_ = [pb(f"ap{n}", [P, CH], f32, ph) for n in range(2)]
        wp_ = [pb(f"wp{n}", [P, CH], f32, ph) for n in range(2)]
        xp_ = [pb(f"xp{n}", [P, CH], f32, ph) for n in range(2)]
        lg = pb("lg", [P, CH], f32, ph)
        cp = pb("cp", [P, 1024], f16, ph)
        (s_xa, s_xc, s_xd, s_xe, s_xb, s_at, s_ah, s_al, s_w, s_y1, s_st, s_mv, s_sd, s_eps, s_rs, s_n, s_xt, s_xh, s_xl, s_lg, s_sig, s_r, s_c0, s_ct, s_cte, s_sel) = S = sems(
            ph, "r_x0", "r_x1", "r_x2", "r_x3", "r_xb", "r_at", "r_ah", "r_al", "r_w", "r_y1", "r_st", "r_mv", "r_sd", "r_epsd", "r_rs", "r_n", "r_xt", "r_xh",
            "r_xl", "r_lg", "r_sig", "r_r", "r_c0", "r_ct", "r_cte", "r_sel")
        s_x = [s_xa, s_xc, s_xd, s_xe]
        x1v = x1[:, :].rearrange("p (i c) -> p i c", c=D)

        ph2 = ExitStack()
        with ph2:
            block = ph2.enter_context(nc.Block())

            @block.sync
            def _(sp):
                for n in range(NC):
                    sp.dma_start(xin[:, n * TPC:(n + 1) * TPC, :],
                                 x[bass.ds(b, 1), n * CH:(n + 1) * CH, :].rearrange("o (i p) c -> p (o i) c", p=P)).then_inc(s_x[n], 16)
                sp.dma_start(sel_w[:, :, :], select).then_inc(s_sel, 16)
                sp.wait_ge(s_sel, 16)

            @block.gpsimd
            def _(pool):
                nc.gpsimd.memset(eps[:, :], EPS).then_inc(s_eps, 1)
                nc.gpsimd.memset(cst[:, :, :], 0.0).then_inc(s_c0, 1)
                pool.wait_ge(s_c0, 1)
                nc.gpsimd.memset(cst[:, :, NE:NX], 1.0).then_inc(s_c0, 1)
                for i in range(NT):
                    if i % TPC == 0:
                        pool.wait_ge(s_x[i // TPC], 16)
                    nc.gpsimd.tensor_tensor(x1v[:, i, :], xin[:, i, :], b_o[:, :], ALU.add).then_inc(s_xb, 1)

            @block.tensor
            def _(pe):
                for s in range(NT + 8):
                    if s < NT:
                        i = s
                        if i >= 2:
                            pe.wait_ge(s_al, i - 1)
                        for c in range(C):
                            mm = nc.tensor.transpose(ap_[i % 2][:, c * P:(c + 1) * P], attn[:, i * D + c * P:i * D + (c + 1) * P], id32[:, :])
                        mm.then_inc(s_at, 1)
                    if 2 <= s < NT + 2:
                        i = s - 2
                        pe.wait_ge(s_al, i + 1)
                        if i >= 2:
                            pe.wait_ge(s_y1, i - 1)
                        n = 0
                        for c in range(C):
                            for part, wh in ((ah, 0), (ah, 1), (al, 0)):
                                mm = nc.tensor.matmul(wp_[i % 2][:, 0:D], part[i % 3][:, c * P:(c + 1) * P], wo_w[:, c, wh * D:(wh + 1) * D],
                                                      start=(n == 0), stop=(n == 3 * C - 1))
                                n += 1
                        mm.then_inc(s_w, 1)
                    if 6 <= s < NT + 6:
                        i = s - 6
                        pe.wait_ge(s_n, i + 1)
                        if i >= 2:
                            pe.wait_ge(s_xl, i - 1)
                        for c in range(C):
                            mm = nc.tensor.transpose(xp_[i % 2][:, c * P:(c + 1) * P], x1[:, i * D + c * P:i * D + (c + 1) * P], id32[:, :])
                        mm.then_inc(s_xt, 1)
                    if s >= 8:
                        i = s - 8
                        pe.wait_ge(s_xl, i + 1)
                        n = 0
                        for c in range(C):
                            for xh, wh in ((0, 0), (0, 1), (1, 0)):
                                mm = nc.tensor.matmul(lg[:, i * NE:(i + 1) * NE], x1t[:, xh, c, i * P:(i + 1) * P], gate_w[:, c, wh, :],
                                                      start=(n == 0), stop=(n == 3 * C - 1))
                                n += 1
                        mm.then_inc(s_lg, 1)
                for half in range(2):
                    pe.wait_ge(s_ct, 2)
                    if half:
                        pe.wait_ge(s_cte, 1)
                    for n in range(8):
                        mm = nc.tensor.transpose(cp[:, n * P:(n + 1) * P], cst[:, half * 8 + n, :], id16[:, :])
                    mm.then_inc(s_lg, 1)

            @block.scalar
            def _(act):
                act.wait_ge(s_eps, 1)
                for s in range(NT + 6):
                    if s < NT:
                        i = s
                        act.wait_ge(s_at, i + 1)
                        if i >= 3:
                            act.wait_ge(s_w, i - 2)
                        nc.scalar.activation(ah[i % 3][:, :], ap_[i % 2][:, 0:D], ACT.Copy).then_inc(s_ah, 1)
                    if 4 <= s < NT + 4:
                        i = s - 4
                        act.wait_ge(s_mv, i + 1)
                        nc.scalar.activation(sd[:, i:i + 1], mv[:, i, 1:2], ACT.Sqrt, bias=eps[:, :]).then_inc(s_sd, 1)
                    if s >= 6:
                        i = s - 6
                        act.wait_ge(s_xt, i + 1)
                        nc.scalar.activation(x1t[:, 0, :, i * P:(i + 1) * P], xp_[i % 2][:, 0:D].rearrange("p (c t) -> p c t", c=C),
                                             ACT.Copy).then_inc(s_xh, 1)
                act.wait_ge(s_lg, NT)
                nc.scalar.activation(score[:, :, :], lg[:, :].rearrange("p (i e) -> p i e", e=NE), ACT.Sigmoid,
                                     scale=1.0 / W_GATE).then_inc(s_sig, 1)
                for half in range(2):
                    act.wait_ge(s_lg, NT + half + 1)
                    nc.scalar.activation(ct[:, half * 1024:(half + 1) * 1024], cp[:, :], ACT.Copy).then_inc(s_cte, 1)

            @block.vector
            def _(dve):
                for s in range(NT + 7):
                    if 5 <= s < NT + 5:
                        i = s - 5
                        dve.wait_ge(s_sd, i + 1)
                        nc.vector.reciprocal(rstd[:, i:i + 1], sd[:, i:i + 1]).then_inc(s_rs, 1)
                    if 1 <= s <= NT:
                        i = s - 1
                        dve.wait_ge(s_ah, i + 1)
                        if i >= 3:
                            dve.wait_ge(s_w, i - 2)
                        nc.vector.tensor_tensor(al[i % 3][:, :], ap_[i % 2][:, 0:D], ah[i % 3][:, :], ALU.subtract).then_inc(s_al, 1)
                    if 5 <= s < NT + 5:
                        i = s - 5
                        dve.wait_ge(s_rs, i + 1)
                        nc.vector.tensor_scalar(x1v[:, i, :], x1v[:, i, :], mv[:, i, 0:1], rstd[:, i:i + 1],
                                                ALU.subtract, ALU.mult).then_inc(s_n, 1)
                    if 3 <= s < NT + 3:
                        i = s - 3
                        dve.wait_ge(s_w, i + 1)
                        dve.wait_ge(s_xb, i + 1)
                        nc.vector.tensor_tensor(x1v[:, i, :], wp_[i % 2][:, 0:D], x1v[:, i, :], ALU.add).then_inc(s_y1, 1)
                    if s >= 7:
                        i = s - 7
                        dve.wait_ge(s_xh, i + 1)
                        nc.vector.tensor_tensor(x1t[:, 1, :, i * P:(i + 1) * P], xp_[i % 2][:, 0:D].rearrange("p (c t) -> p c t", c=C),
                                                x1t[:, 0, :, i * P:(i + 1) * P], ALU.subtract).then_inc(s_xl, 1)
                    if 3 <= s < NT + 3:
                        i = s - 3
                        dve.wait_ge(s_y1, i + 1)
                        nc.vector.bn_stats(st[:, i, :], x1v[:, i, :]).then_inc(s_st, 1)
                        dve.wait_ge(s_st, i + 1)
                        nc.vector.bn_aggr(mv[:, i, :], st[:, i, :]).then_inc(s_mv, 1)

                done = [0]

                def link(op):
                    done[0] += 1
                    op.then_inc(s_r, 1)
                    dve.wait_ge(s_r, done[0])

                V = nc.vector
                dve.wait_ge(s_sig, 1)
                link(V.tensor_tensor(bsc[:, :, :], score[:, :, :], b_e[:, :].rearrange("p (o e) -> p o e", o=1).to_broadcast([P, NT, NE]), ALU.add))
                pr = bsc[:, :, :].rearrange("p i (g a e) -> p (i g) a e", a=2, e=2)
                pm, p2 = (t[:, :, :, :].rearrange("p i g a -> p (i g) a") for t in (pmax, psum2))
                link(V.tensor_tensor(pm, pr[:, :, :, 0], pr[:, :, :, 1], ALU.max))
                link(V.tensor_tensor(p2, pr[:, :, :, 0], pr[:, :, :, 1], ALU.add))
                gv, g2 = (t[:, :, :].rearrange("p i g -> p (i g)") for t in (gsc, gs2))
                link(V.tensor_tensor(gv, pm[:, :, 0], pm[:, :, 1], ALU.add))
                link(V.tensor_tensor(g2, p2[:, :, 0], p2[:, :, 1], ALU.max))
                link(V.tensor_tensor(gv, gv, g2, ALU.max))
                for i in range(NT):
                    op = V.max(gtop[:, i, :], gsc[:, i, :])
                    op.then_inc(s_r, 1)
                done[0] += NT
                dve.wait_ge(s_r, done[0])
                link(V.memset(gtop[:, :, TOPG:8], BIG))
                for i in range(NT):
                    V.match_replace(grep[:, i, :], gtop[:, i, :], gsc[:, i, :], -BIG).then_inc(s_r, 1)
                done[0] += NT
                dve.wait_ge(s_r, done[0])
                link(V.tensor_scalar(gsel[:, :, :], grep[:, :, :], -BIG, None, ALU.is_equal))
                link(V.tensor_tensor(masked[:, :, :].rearrange("p i (g e) -> p (i g) e", e=EPG), bsc[:, :, :].rearrange("p i (g e) -> p (i g) e", e=EPG),
                                     gsel[:, :, :].rearrange("p i (g o) -> p (i g) o", o=1).to_broadcast([P, NT * NGR, EPG]), ALU.mult))
                for i in range(NT):
                    V.max(etop[:, i, :], masked[:, i, :]).then_inc(s_r, 1)
                done[0] += NT
                dve.wait_ge(s_r, done[0])
                link(V.memset(etop[:, :, TOPK:8], BIG))
                for i in range(NT):
                    V.match_replace(erep[:, i, :], etop[:, i, :], masked[:, i, :], -BIG).then_inc(s_r, 1)
                done[0] += NT
                dve.wait_ge(s_r, done[0])
                link(V.scalar_tensor_tensor(out=wgt[:, :, :].rearrange("p i e -> p (i e)"), in0=erep[:, :, :].rearrange("p i e -> p (i e)"), scalar=-BIG,
                                            in1=score[:, :, :].rearrange("p i e -> p (i e)"), op0=ALU.is_equal, op1=ALU.mult))
                link(V.reduce_sum(wsum[:, :], wgt[:, :, :], AX.X))
                link(V.tensor_scalar(wsum[:, :], wsum[:, :], 1e-20, None, ALU.add))
                link(V.reciprocal(wsum[:, :], wsum[:, :]))
                link(V.scalar_tensor_tensor(out=wgt[:, :, :], in0=wgt[:, :, :], scalar=2.5,
                                            in1=wsum[:, :].rearrange("p (i o) -> p i o", o=1).to_broadcast([P, NT, NE]), op0=ALU.mult, op1=ALU.mult))
                dve.wait_ge(s_c0, 2)
                V.tensor_copy(cst[:, :, 0:NE], wgt[:, :, :]).then_inc(s_ct, 1)
                dve.wait_ge(s_ct, 1)
                V.tensor_tensor(cst[:, :, NX:NX + NE], wgt[:, :, :], cst[:, :, 0:NE], ALU.subtract).then_inc(s_ct, 1)
        retire(S)


def experts(nc, sb, pb, sems, retire, b, up_w, dn_w, sel_w, x1, x1t, ct, out):
    f32, f16 = mybir.dt.float32, mybir.dt.float16
    ACT = mybir.ActivationFunctionType
    NB, SKEW = 4, 2
    STEPS = NC * NX
    ph = ExitStack()
    with ph:
        r = [sb(f"e_r{k}", [P, CH], f32, ph) for k in range(NB)]
        r2 = [sb(f"e_r2{k}", [P, CH], f32, ph) for k in range(NB)]
        h = [sb(f"e_h{k}", [P, CH], f32, ph) for k in range(NB)]
        hh = [sb(f"e_hh{k}", [P, CH], f16, ph) for k in range(NB)]
        hl = [sb(f"e_hl{k}", [P, CH], f16, ph) for k in range(NB)]
        st = sb("e_st", [P, TPC, 6], f32, ph)
        mv = sb("e_mv", [P, TPC, 2], f32, ph)
        eps = sb("e_eps", [P, 1], f32, ph)
        sd = sb("e_sd", [P, TPC], f32, ph)
        rstd = sb("e_rstd", [P, TPC], f32, ph)
        yo = [sb(f"e_yo{k}", [P, TPC, D], f32, ph) for k in range(2)]
        z = [pb(f"e_z{k}", [P, CH], f32, ph) for k in range(2)]
        cb = [pb(f"e_cb{k}", [P, CH], f32, ph) for k in range(2)]
        o = [[pb(f"e_o{n}{k}", [P, 2 * D], f32, ph) for k in range(2)] for n in range(2)]
        (s_z, s_r, s_r2, s_cb, s_h, s_hi, s_lo, s_dn, s_t2, s_st, s_mv, s_sd, s_eps, s_rs, s_n, s_out0, s_out1) = S = sems(
            ph, "e_z", "e_r", "e_r2", "e_cb", "e_h", "e_hi", "e_lo", "e_dn", "e_t2", "e_st", "e_mv", "e_sd", "e_epsd", "e_rs",
            "e_n", "e_out0", "e_out1")
        s_out = [s_out0, s_out1]
        un = 1.0 / (H_SCALE * W_DN)
        x1v = x1[:, :].rearrange("p (i c) -> p i c", c=D)
        outv = out.rearrange("b (i p) c -> p (b i) c", p=P)

        def weighted(s):
            return s // NX * NE + min(s % NX, NE)

        def stage(s, n):
            c, e = divmod(s - SKEW - n, NX)
            return c - 1 if e == 0 and 1 <= c <= NC else None

        ph2 = ExitStack()
        with ph2:
            block = ph2.enter_context(nc.Block())

            @block.tensor
            def _(pe):
                for s in range(STEPS + SKEW):
                    if s < STEPS:
                        n, e = divmod(s, NX)
                        w = weighted(s)
                        if s >= 2:
                            pe.wait_ge(s_r, s - 1)
                        k = 0
                        for c in range(C):
                            for xh, wh in ((0, 0), (1, 0), (0, 1)):
                                mm = nc.tensor.matmul(z[s % 2][:, :], up_w[:, e, c, wh, :], x1t[:, xh, c, n * CH:(n + 1) * CH],
                                                      start=(k == 0), stop=(k == 3 * C - 1))
                                k += 1
                        mm.then_inc(s_z, 1)
                        if e < NE:
                            if w >= 2:
                                pe.wait_ge(s_h, w - 1)
                            nc.tensor.matmul(cb[w % 2][:, :], sel_w[:, e, :], ct[:, n * CH:(n + 1) * CH],
                                             start=True, stop=True).then_inc(s_cb, 1)
                    if s >= SKEW:
                        d = s - SKEW
                        n, e = divmod(d, NX)
                        pe.wait_ge(s_lo, d + 1)
                        if e == 0 and n >= 2:
                            pe.wait_ge(s_t2, 2 * (n - 1))
                        for k in range(TPC):
                            bank, at = o[n % 2][k // 2], k % 2 * D
                            for q, (part, wh) in enumerate(((hh, 0), (hh, 1), (hl, 0))):
                                mm = nc.tensor.matmul(bank[:, at:at + D], part[d % NB][:, k * P:(k + 1) * P], dn_w[:, e, wh * D:(wh + 1) * D],
                                                      start=(e == 0 and k % 2 == 0 and q == 0), stop=(e == NX - 1 and k % 2 == 1 and q == 2))
                        mm.then_inc(s_dn, 1)

            @block.scalar
            def _(act):
                act.wait_ge(s_eps, 1)
                for s in range(STEPS + SKEW + 4):
                    if s < STEPS:
                        act.wait_ge(s_z, s + 1)
                        if s >= NB:
                            act.wait_ge(s_r2, s - NB + 1)
                        nc.scalar.activation(r[s % NB][:, :], z[s % 2][:, :], ACT.Relu, scale=H_SCALE ** 0.5 / W_UP).then_inc(s_r, 1)
                    if 1 <= s <= STEPS:
                        d = s - 1
                        if d % NX < NE:
                            act.wait_ge(s_h, weighted(d) + 1)
                            src = h
                        else:
                            act.wait_ge(s_r2, d + 1)
                            src = r2
                        if d >= NB:
                            act.wait_ge(s_dn, d - NB + 1)
                        nc.scalar.activation(hh[d % NB][:, :], src[d % NB][:, :], ACT.Copy).then_inc(s_hi, 1)
                    n = stage(s, 3)
                    if n is not None:
                        act.wait_ge(s_mv, TPC * (n + 1))
                        if n:
                            act.wait_ge(s_rs, n)
                        nc.scalar.activation(sd[:, :], mv[:, :, 1], ACT.Sqrt, bias=eps[:, :]).then_inc(s_sd, 1)

            @block.gpsimd
            def _(pool):
                nc.gpsimd.memset(eps[:, :], EPS).then_inc(s_eps, 1)
                for s in range(STEPS):
                    pool.wait_ge(s_r, s + 1)
                    if s >= NB:
                        pool.wait_ge(s_lo, s - NB + 1)
                    nc.gpsimd.tensor_tensor(r2[s % NB][:, :], r[s % NB][:, :], r[s % NB][:, :], ALU.mult).then_inc(s_r2, 1)

            @block.vector
            def _(dve):
                for s in range(STEPS + SKEW + 6):
                    if 1 <= s <= STEPS:
                        d = s - 1
                        dve.wait_ge(s_hi, d + 1)
                        if d >= NB:
                            dve.wait_ge(s_dn, d - NB + 1)
                        src = h if d % NX < NE else r2
                        nc.vector.tensor_tensor(hl[d % NB][:, :], src[d % NB][:, :], hh[d % NB][:, :], ALU.subtract).then_inc(s_lo, 1)
                    if s < STEPS and s % NX < NE:
                        w = weighted(s)
                        dve.wait_ge(s_r2, s + 1)
                        dve.wait_ge(s_cb, w + 1)
                        if s >= NB:
                            dve.wait_ge(s_lo, s - NB + 1)
                        nc.vector.tensor_tensor(h[s % NB][:, :], r2[s % NB][:, :], cb[w % 2][:, :], ALU.mult).then_inc(s_h, 1)
                    n = stage(s, 0)
                    if n is not None:
                        dve.wait_ge(s_dn, (n + 1) * NX)
                        for q in range(2):
                            xr = x1[:, (n * TPC + 2 * q) * D:(n * TPC + 2 * q + 2) * D]
                            nc.vector.scalar_tensor_tensor(out=xr, in0=o[n % 2][q][:, :], scalar=un, in1=xr,
                                                           op0=ALU.mult, op1=ALU.add).then_inc(s_t2, 1)
                    n = stage(s, 2)
                    if n is not None:
                        dve.wait_ge(s_t2, 2 * (n + 1))
                        for k in range(TPC):
                            nc.vector.bn_stats(st[:, k, :], x1v[:, n * TPC + k, :]).then_inc(s_st, 1)
                        for k in range(TPC):
                            dve.wait_ge(s_st, TPC * n + k + 1)
                            nc.vector.bn_aggr(mv[:, k, :], st[:, k, :]).then_inc(s_mv, 1)
                    n = stage(s, 4)
                    if n is not None:
                        dve.wait_ge(s_sd, n + 1)
                        nc.vector.reciprocal(rstd[:, :], sd[:, :]).then_inc(s_rs, 1)
                        dve.wait_ge(s_rs, n + 1)
                        if n >= 2:
                            dve.wait_ge(s_out[n % 2], 16 * (n // 2))
                        for k in range(TPC):
                            nc.vector.tensor_scalar(yo[n % 2][:, k, :], x1v[:, n * TPC + k, :], mv[:, k, 0:1], rstd[:, k:k + 1],
                                                    ALU.subtract, ALU.mult).then_inc(s_n, 1)

            @block.sync
            def _(sp):
                for n in range(NC):
                    sp.wait_ge(s_n, TPC * (n + 1))
                    sp.dma_start(outv[:, bass.ds(b * NT + n * TPC, TPC), :], yo[n % 2][:, :, :]).then_inc(s_out[n % 2], 16)
                for k in range(2):
                    sp.wait_ge(s_out[k], 16 * (NC // 2))
        retire(S)


def kernel(**inputs):
    import ml_dtypes
    import concourse.bacc as _bacc
    from concourse.bass_utils import run_bass_kernel_spmd as _run

    a = {k.removeprefix("L0_"): np.asarray(v) for k, v in inputs.items()}

    def rows(w):
        return w.reshape(C, P, -1).transpose(1, 0, 2)

    def every(v):
        return np.broadcast_to(v.reshape(1, -1), (P, v.size))

    up = np.concatenate([a["ffn_up_w"], a["ffn_shared_up_w"].reshape(NSH // FI, FI, D)])
    down = np.concatenate([a["ffn_down_w"], a["ffn_shared_down_w"].reshape(D, NSH // FI, FI).transpose(1, 0, 2)])
    arrays = {
        "x": a["attn_x"],
        "xt": a["attn_x"].reshape(B, T, C, P).transpose(0, 3, 2, 1),
        "wqkv": rows(np.concatenate([a["attn_Wq"], a["attn_Wk"], a["attn_Wv"]], axis=1)),
        "bqkv": every(np.concatenate([a["attn_bq"], a["attn_bk"], a["attn_bv"]])),
        "wo": rows(a["attn_Wo"]),
        "bo": every(a["attn_bo"]),
        "gate": rows(a["ffn_gate_w"].T),
        "ebias": every(a["ffn_e_bias"]),
        "up": up.reshape(NX, FI, C, P).transpose(3, 0, 2, 1),
        "down": down.transpose(2, 0, 1),
    }
    pos = np.arange(T, dtype=np.float32)[:, None]
    freq = np.exp(-(np.arange(0, DH, 2, dtype=np.float32) / DH) * np.log(np.float32(10000.0)))
    angle = pos * freq
    cos = np.repeat(np.cos(angle), 2, axis=1)
    sin = np.stack([-np.sin(angle), np.sin(angle)], axis=-1).reshape(T, DH)
    tiles = lambda t: t.reshape(NT, P, DH).transpose(1, 0, 2).astype(np.float32)
    select = np.zeros((P, NX, P), np.float16)
    for e in range(NX):
        select[e, e] = select[NX + e, e] = 1.0
    arrays |= {
        "rope_cos": tiles(cos), "rope_sin": tiles(sin),
        "eye32": np.eye(P, dtype=np.float32), "eye16": np.eye(P, dtype=np.float16), "eyeb": np.eye(P, dtype=ml_dtypes.bfloat16),
        "future": np.where(np.arange(P)[None, :] > np.arange(P)[:, None], -1e30, 0.0).astype(ml_dtypes.bfloat16),
        "select": select,
    }
    nc = _bacc.Bacc("TRN2", target_bir_lowering=False, num_devices=1)
    aps = {}
    for name, v in arrays.items():
        arrays[name] = v = np.ascontiguousarray(v)
        aps[name] = nc.dram_tensor(name, v.shape, mybir.dt.from_np(v.dtype), kind="ExternalInput").ap()
    aps["out"] = nc.dram_tensor("out", (B, T, D), mybir.dt.float32, kind="ExternalOutput").ap()
    nc.disable_value_cache = True
    layer(nc, **aps)
    return _run(nc, [arrays], core_ids=[0]).results[0]["out"]
```

```python
import numpy as np
import concourse.bass as bass
from concourse import mybir
from concourse.alu_op_type import AluOpType as ALU
from contextlib import ExitStack

B, T, D = 4, 2048, 256
NH, NG, DH = 16, 4, 16
HPG = NH // NG
NE, FI, NSH = 32, 128, 512
NX = NE + NSH // FI
NGR, EPG, TOPG, TOPK = 8, 4, 4, 6
EPS = 1e-5
P = 128
C = D // P
NT = T // P
CH = 512
TPC = CH // P
NC = T // CH
QKV = D + 2 * NG * DH
QK = D + NG * DH
ROW = 3 * DH
M_ROW = 2 * ROW
M_ONE = 64.0
W_UP, W_DN, W_GATE, H_SCALE = 64.0, 64.0, 16.0, 16.0
BIG = 3.0e38
FIRST, LIMIT, RAMP, RATE_FIRST, RATE, CARRY = 8, 96, 200, 0.92, 0.85, 600


def layer(nc, x, xt, wqkv, bqkv, wo, bo, gate, ebias, up, down, rope_cos, rope_sin,
          eye32, eye16, eyeb, future, select, out):
    f32, f16, bf16 = mybir.dt.float32, mybir.dt.float16, mybir.dt.bfloat16
    ACT = mybir.ActivationFunctionType

    ctx = ExitStack()
    with ctx:
        def sb(name, shape, dt, where=ctx):
            return where.enter_context(nc.sbuf_tensor(name, shape, dt))

        def pb(name, shape, dt, where):
            return where.enter_context(nc.psum_tensor(name, shape, dt))

        def sems(where, *names):
            return [where.enter_context(nc.semaphore(n)) for n in names]

        up_w = sb("up_w", [P, NX, C, 2, FI], f16)
        dn_w = sb("dn_w", [P, NX, 2 * D], f16)
        qkv_w = sb("qkv_w", [P, C, 2, QKV], f16)
        wo_w = sb("wo_w", [P, C, 2 * D], f16)
        gate_w = sb("gate_w", [P, C, 2, NE], f16)
        b_o = sb("b_o", [P, D], f32)
        b_e = sb("b_e", [P, NE], f32)
        id32 = sb("id32", [P, P], f32)
        id16 = sb("id16", [P, P], f16)
        idb = sb("idb", [P, P], bf16)
        fut = sb("fut", [P, P], bf16)
        attn = sb("attn", [P, NT * D], f32)
        xhl = attn[:, :].bitcast(f16).rearrange("p (s c t) -> p s c t", s=2, c=C)

        def retire(names):
            numbers = [s.num for s in names]
            assert numbers == list(range(numbers[0], numbers[0] + len(numbers)))
            nc.all_engine_barrier(sems_to_clear=range(numbers[0], numbers[0] + len(numbers)))

        st = ExitStack()
        with st:
            w_stage = sb("w_stage", [P, 2 * NX * C * FI], f32, st)
            s_stage = sb("s_stage", [P, C * (QKV + D + NE)], f32, st)
            n_up = NX * C * FI
            qo, oo, go = 0, C * QKV, C * (QKV + D)
            PIECES = 4
            s_const, s_small, s_whi, s_wlo, *s_piece = S = sems(
                st, "s_const", "s_small", "s_whi", "s_wlo", *(f"s_w{n}" for n in range(2 * PIECES)))
            consts = [(b_o[:, :], bo),
                      (b_e[:, :], ebias), (id32[:, :], eye32), (id16[:, :], eye16), (idb[:, :], eyeb),
                      (fut[:, :], future)]
            splits = [
                (s_small, w_v(s_stage[:, qo:oo], QKV), 1.0, qkv_w[:, :, 0, :], qkv_w[:, :, 1, :]),
                (s_small, w_v(s_stage[:, oo:go], D), 1.0, wo_w[:, :, 0:D], wo_w[:, :, D:2 * D]),
                (s_small, w_v(s_stage[:, go:go + C * NE], NE), W_GATE, gate_w[:, :, 0, :], gate_w[:, :, 1, :]),
            ]
            loads = []
            for n in range(PIECES):
                e0, e1 = n * NX // PIECES, (n + 1) * NX // PIECES
                for s, src, at, scale, shape, hi, lo in (
                        (s_piece[2 * n], up, 0, W_UP, "p e c i -> p (e c) i", up_w[:, e0:e1, :, 0, :], up_w[:, e0:e1, :, 1, :]),
                        (s_piece[2 * n + 1], down, n_up, W_DN, None, dn_w[:, e0:e1, 0:D], dn_w[:, e0:e1, D:2 * D])):
                    stage = w_stage[:, at + e0 * C * FI:at + e1 * C * FI]
                    if shape:
                        loads.append((s, stage.rearrange("p (e c i) -> p e c i", c=C, i=FI), src[:, e0:e1, :, :]))
                        splits.append((s, stage.rearrange("p (e i) -> p e i", i=FI), scale, hi.rearrange(shape), lo.rearrange(shape)))
                    else:
                        loads.append((s, stage.rearrange("p (e i) -> p e i", i=D), src[:, e0:e1, :]))
                        splits.append((s, stage.rearrange("p (e i) -> p e i", i=D), scale, hi, lo))
            block = st.enter_context(nc.Block())

            @block.sync
            def _(sp):
                sp.dma_start(s_stage[:, qo:oo], wqkv).then_inc(s_small, 16)
                sp.dma_start(s_stage[:, oo:go], wo).then_inc(s_small, 16)
                sp.dma_start(s_stage[:, go:go + C * NE], gate).then_inc(s_small, 16)
                for s, dst, src in loads:
                    sp.dma_start(dst, src).then_inc(s, 16)
                for dst, src in consts:
                    sp.dma_start(dst, src).then_inc(s_const, 16)
                sp.wait_ge(s_const, 16 * len(consts))

            @block.scalar
            def _(act):
                for s, src, scale, hi, _lo in splits:
                    act.wait_ge(s, 48 if s is s_small else 16)
                    nc.scalar.activation(hi, src, ACT.Copy, scale=scale).then_inc(s_whi, 1)

            @block.vector
            def _(dve):
                for n, (s, src, scale, hi, lo) in enumerate(splits):
                    dve.wait_ge(s_whi, n + 1)
                    nc.vector.scalar_tensor_tensor(out=lo, in0=src, scalar=scale, in1=hi,
                                                   op0=ALU.mult, op1=ALU.subtract).then_inc(s_wlo, 1)
                dve.wait_ge(s_wlo, len(splits))
            del block
        retire(S)

        with nc.Fori(0, B) as b:
            qkv_ctx = ExitStack()
            with qkv_ctx:
                qs = sb("qs", [P, (NH // 2) * T], f16, qkv_ctx)
                ks = sb("ks", [P, 2 * NG * T], f16, qkv_ctx)
                vs = sb("vs", [P, NG, NT, 32], f32, qkv_ctx)
                project(nc, sb, pb, sems, retire, b, xt, xhl, qkv_w, bqkv, rope_cos, rope_sin, id16, qs, ks, vs)
                attend(nc, sb, pb, sems, retire, qs, ks, vs, attn, id32, id16, idb, fut)
            ffn_ctx = ExitStack()
            with ffn_ctx:
                x1 = sb("x1", [P, NT * D], f32, ffn_ctx)
                x1t = sb("x1t", [P, 2, C, T], f16, ffn_ctx)
                ct = sb("ct", [P, T], f16, ffn_ctx)
                sel_w = sb("sel_w", [P, NX, P], f16, ffn_ctx)
                score = sb("score", [P, NT, NE], f32, ffn_ctx)
                route(nc, sb, pb, sems, retire, b, x, select, sel_w, attn, wo_w, b_o, gate_w, id32, x1, x1t, score)
                experts(nc, sb, pb, sems, retire, b, up_w, dn_w, sel_w, b_e, id16, x1, x1t, score, ct, out)


def w_v(ap, width):
    return ap.rearrange("p (c n) -> p c n", n=width)


def project(nc, sb, pb, sems, retire, b, xt, xhl, qkv_w, bqkv, rope_cos, rope_sin, id16, qs, ks, vs):
    f32, f16 = mybir.dt.float32, mybir.dt.float16
    ACT = mybir.ActivationFunctionType
    NHI = 4
    NQ = 3
    ph = ExitStack()
    with ph:
        xs = [sb(f"xs{n}", [P, C, CH], f32, ph) for n in range(2)]
        qkv = [sb(f"qkv{n}", [P, QKV], f32, ph) for n in range(2)]
        rc = [sb(f"rc{n}", [P, QK], f32, ph) for n in range(2)]
        rs = [sb(f"rs{n}", [P, QK], f32, ph) for n in range(2)]
        rot = [sb(f"rot{n}", [P, QK], f32, ph) for n in range(2)]
        qt = [sb(f"qt{n}", [P, (NH // 2) * P], f16, ph) for n in range(NQ)]
        kt = [sb(f"kt{n}", [P, NG * 2 * P], f16, ph) for n in range(NQ)]
        cos_t = sb("cos_t", [P, NT, DH], f32, ph)
        sin_t = sb("sin_t", [P, NT, DH], f32, ph)
        b_qkv = sb("b_qkv", [P, QKV], f32, ph)
        pj = [pb(f"pj{n}", [P, 512], f32, ph) for n in range(2)]
        tq = [pb(f"tq{n}", [P, 1024], f16, ph) for n in range(2)]
        tk = [pb(f"tk{n}", [P, 1024], f16, ph) for n in range(2)]
        (s_x0, s_x1, s_xhi, s_xlo, s_proj, s_qkv, s_rc, s_rs, s_rot, s_hi, s_v, s_lo, s_tr, s_tqe, s_tke, s_set, s_tab, s_klo) = S = sems(
            ph, "p_x0", "p_x1", "p_xhi", "p_xlo", "p_proj", "p_qkv", "p_rc", "p_rs", "p_rot", "p_hi", "p_v", "p_lo",
            "p_tr", "p_tqe", "p_tke", "p_set", "p_tab", "p_klo")
        s_x = [s_x0, s_x1]
        qsv = qs[:, :].rearrange("p (j t) -> p j t", t=T)
        ksv = ks[:, :].rearrange("p (j t) -> p j t", t=T)

        def heads(ap):
            return ap.rearrange("p (h d) -> p h d", d=DH)

        def q_rows(n, at):
            return qt[n][:, :].rearrange("p (j r) -> p j r", r=P)[:, :, 0:2 * ROW].rearrange("p j (e r) -> p j e r", e=2)[:, :, :, at:at + DH]

        def k_both(n, at):
            kr = kt[n][:, :].rearrange("p (g c) -> p g c", g=NG)
            return bass.AP(kr.tensor, kr.offset + at, [kr.ap[0], [2 * P, NG], [P + ROW, 2], [1, DH]])

        def k_twice(i):
            return rot[i % 2][:, D:QK].rearrange("p (g o d) -> p g o d", g=NG, o=1).to_broadcast([P, NG, 2, DH])

        def pairs(ap):
            return ap.rearrange("p (j e d) -> p j e d", e=2, d=DH)

        ph2 = ExitStack()
        with ph2:
            block = ph2.enter_context(nc.Block())

            @block.sync
            def _(sp):
                for c in range(NC):
                    if c >= 2:
                        sp.wait_ge(s_xlo, c - 1)
                    sp.dma_start(xs[c % 2][:, :, :], xt[bass.ds(b, 1), :, :, c * CH:(c + 1) * CH].rearrange("o p c t -> p (o c) t")
                                 ).then_inc(s_x[c % 2], 16)
                    if c == 0:
                        for dst, src in ((b_qkv[:, :], bqkv), (cos_t[:, :, :], rope_cos), (sin_t[:, :, :], rope_sin)):
                            sp.dma_start(dst, src).then_inc(s_tab, 16)

            @block.tensor
            def _(pe):
                for s in range(NT + 3):
                    if s < NT:
                        i = s
                        pe.wait_ge(s_xlo, i // TPC + 1)
                        if i >= 2:
                            pe.wait_ge(s_qkv, i - 1)
                        n = 0
                        for c in range(C):
                            for xp, wp in ((0, 0), (0, 1), (1, 0)):
                                mm = nc.tensor.matmul(pj[i % 2][:, 0:QKV], xhl[:, xp, c, i * P:(i + 1) * P], qkv_w[:, c, wp, :],
                                                      start=(n == 0), stop=(n == 3 * C - 1))
                                n += 1
                        mm.then_inc(s_proj, 1)
                    if s >= 3:
                        i = s - 3
                        pe.wait_ge(s_lo, i + 1)
                        pe.wait_ge(s_klo, i + 1)
                        if i >= 2:
                            pe.wait_ge(s_tqe, i - 1)
                            pe.wait_ge(s_tke, i - 1)
                        for j in range(8):
                            nc.tensor.transpose(tq[i % 2][:, j * P:(j + 1) * P], qt[i % NQ][:, j * P:(j + 1) * P], id16[:, :])
                        for j in range(8):
                            mm = nc.tensor.transpose(tk[i % 2][:, j * P:(j + 1) * P], kt[i % NQ][:, j * P:(j + 1) * P], id16[:, :])
                        mm.then_inc(s_tr, 1)

            @block.gpsimd
            def _(pool):
                for n in range(NQ):
                    nc.gpsimd.memset(qt[n][:, :].bitcast(f32), 0.0).then_inc(s_set, 1)
                    nc.gpsimd.memset(kt[n][:, :].bitcast(f32), 0.0).then_inc(s_set, 1)
                pool.wait_ge(s_set, 2 * NQ)
                for n in range(NQ):
                    for par in range(2):
                        at = par * P + M_ROW + 2 * par
                        ones = kt[n][:, :].rearrange("p (g c) -> p g c", g=NG)[:, :, at:at + 2]
                        nc.gpsimd.memset(ones, M_ONE).then_inc(s_set, 1)
                nc.gpsimd.memset(vs[:, :, :, DH:32], 1.0).then_inc(s_set, 1)
                def split(c):
                    pool.wait_ge(s_xhi, c + 1)
                    pool.wait_ge(s_xlo, c)
                    nc.gpsimd.tensor_tensor(xhl[:, 1, :, c * CH:(c + 1) * CH], xs[c % 2][:, :, :],
                                            xhl[:, 0, :, c * CH:(c + 1) * CH], ALU.subtract).then_inc(s_xlo, 1)

                pool.wait_ge(s_tab, 48)
                for s in range(NT + 2):
                    if s >= 2:
                        i = s - 2
                        pool.wait_ge(s_hi, NHI * (i + 1))
                        nc.gpsimd.tensor_tensor(k_both(i % NQ, DH), k_twice(i), k_both(i % NQ, 0), ALU.subtract).then_inc(s_klo, 1)
                    if s >= NT:
                        continue
                    i = s
                    pool.wait_ge(s_qkv, i + 1)
                    if i >= 2:
                        pool.wait_ge(s_rot, i - 1)
                    for o in range(2):
                        src = qkv[i % 2][:, 0:QK].rearrange("p (h d e) -> p h d e", e=2, d=DH // 2)[:, :, :, 1 - o]
                        dst = rs[i % 2][:, :].rearrange("p (h d e) -> p h d e", e=2, d=DH // 2)[:, :, :, o]
                        sn = sin_t[:, i:i + 1, :].rearrange("p o (d e) -> p o d e", e=2)[:, :, :, o].to_broadcast([P, NH + NG, DH // 2])
                        nc.gpsimd.tensor_tensor(dst, src, sn, ALU.mult).then_inc(s_rs, 1)
                    if s % TPC == 0 and s // TPC + 1 < NC:
                        split(s // TPC + 1)

            @block.scalar
            def _(act):
                def split(c):
                    act.wait_ge(s_x[c % 2], 16 * (c // 2 + 1))
                    nc.scalar.activation(xhl[:, 0, :, c * CH:(c + 1) * CH], xs[c % 2][:, :, :], ACT.Copy).then_inc(s_xhi, 1)

                split(0)
                split(1)
                act.wait_ge(s_set, 4 * NQ)
                for s in range(1, NT + 4):
                    if s >= 4:
                        i = s - 4
                        act.wait_ge(s_tr, i + 1)
                        nc.scalar.activation(ksv[:, :, i * P:(i + 1) * P], tk[i % 2][:, :].rearrange("p (j t) -> p j t", t=P),
                                             ACT.Copy).then_inc(s_tke, 1)
                    if s - 1 < NT:
                        i = s - 1
                        act.wait_ge(s_qkv, i + 1)
                        nc.scalar.activation(vs[:, :, i, 0:DH], qkv[i % 2][:, QK:QKV].rearrange("p (g d) -> p g d", d=DH), ACT.Copy).then_inc(s_v, 1)
                        act.wait_ge(s_rot, i + 1)
                        if i >= NQ:
                            act.wait_ge(s_tr, i - NQ + 1)
                        qh = pairs(rot[i % 2][:, 0:D])
                        kh = k_twice(i)
                        nc.scalar.activation(q_rows(i % NQ, 0), qh, ACT.Copy).then_inc(s_hi, 1)
                        nc.scalar.activation(q_rows(i % NQ, DH), qh, ACT.Copy).then_inc(s_hi, 1)
                        for at in (0, 2 * DH):
                            nc.scalar.activation(k_both(i % NQ, at), kh, ACT.Copy).then_inc(s_hi, 1)
                    if s % TPC == 1 and s // TPC + 2 < NC:
                        split(s // TPC + 2)

            @block.vector
            def _(dve):
                dve.wait_ge(s_xhi, 1)
                nc.vector.tensor_tensor(xhl[:, 1, :, 0:CH], xs[0][:, :, :], xhl[:, 0, :, 0:CH], ALU.subtract).then_inc(s_xlo, 1)
                dve.wait_ge(s_tab, 48)
                for s in range(NT + 4):
                    if s >= 4:
                        i = s - 4
                        dve.wait_ge(s_tr, i + 1)
                        nc.vector.tensor_copy(qsv[:, :, i * P:(i + 1) * P],
                                              tq[i % 2][:, :].rearrange("p (j t) -> p j t", t=P)).then_inc(s_tqe, 1)
                    if s < NT:
                        i = s
                        dve.wait_ge(s_proj, i + 1)
                        if i >= 2:
                            dve.wait_ge(s_v, i - 1)
                            dve.wait_ge(s_rs, 2 * (i - 1))
                        nc.vector.tensor_tensor(qkv[i % 2][:, :], pj[i % 2][:, 0:QKV], b_qkv[:, :], ALU.add).then_inc(s_qkv, 1)
                    if 2 <= s < NT + 2:
                        i = s - 2
                        dve.wait_ge(s_hi, NHI * i + 2)
                        nc.vector.tensor_tensor(q_rows(i % NQ, 2 * DH), pairs(rot[i % 2][:, 0:D]), q_rows(i % NQ, 0),
                                                ALU.subtract).then_inc(s_lo, 1)
                    if 1 <= s <= NT:
                        i = s - 1
                        dve.wait_ge(s_rs, 2 * (i + 1))
                        dve.wait_ge(s_rc, i + 1)
                        if i >= 2:
                            dve.wait_ge(s_hi, NHI * (i - 1))
                            dve.wait_ge(s_lo, i - 1)
                            dve.wait_ge(s_klo, i - 1)
                        nc.vector.tensor_tensor(rot[i % 2][:, :], rc[i % 2][:, :], rs[i % 2][:, :], ALU.add).then_inc(s_rot, 1)
                    if s < NT:
                        i = s
                        dve.wait_ge(s_qkv, i + 1)
                        if i >= 2:
                            dve.wait_ge(s_rot, i - 1)
                        cs = cos_t[:, i:i + 1, :].to_broadcast([P, NH + NG, DH])
                        nc.vector.tensor_tensor(heads(rc[i % 2][:, :]), heads(qkv[i % 2][:, 0:QK]), cs, ALU.mult).then_inc(s_rc, 1)
        retire(S)


def attend(nc, sb, pb, sems, retire, qs, ks, vs, attn, id32, id16, idb, fut):
    f32, f16 = mybir.dt.float32, mybir.dt.float16
    ACT = mybir.ActivationFunctionType
    AX = mybir.AxisListType
    NP, NSC, NMX = 4, 3, 3
    SKEW = 2
    ORDER = ((0, 0.2), (1, 0.4), (None, 0.6), (2, 0.8), (3, 1.0))

    CHUNKS = [(0, 0), (1, 0), (0, 1), (0, 2), (0, 3), (1, 3), (1, 2), (2, 3), (2, 2), (3, 3), (3, 2), (1, 1), (2, 1), (3, 1), (2, 0), (3, 0)]
    QGR, QCH = [g for g, _ in CHUNKS], [q for _, q in CHUNKS]
    units = []
    steps = []
    done = []
    for c in range(NG * NC):
        J = QCH[c]
        for tt in range(TPC):
            width = (J * TPC + tt + 1) * P
            for h in range(HPG):
                for n in range(-(-width // CH)):
                    w = min(CH, width - n * CH)
                    units.append((c, tt, h, n, n * CH, w, n * CH + w == width))
        done.append(len(units))
        steps += [(c, j) for j in range(TPC * (J + 1))]

    starts = [steps.index((c, 0)) for c in range(len(done))]
    def pe_unit(n):
        return units[n][5] / 2.4 + (P / 2.4 if units[n][6] else 0)

    def dve_unit(n):
        return units[n][5] / 0.96 + 65

    plan = []
    first = done[0] + FIRST
    over = 0.0
    n = first
    for k, (c, j) in enumerate(steps):
        w = CH - max(0, j - TPC * QCH[c]) * P
        time, reduced, a = HPG * w * (1 + 1.1) / 2.4 + 100, over, n
        rate = RATE if n > RAMP else RATE_FIRST
        due = max([done[x] for x in range(len(done)) if starts[x] - (TPC if x > 1 else 2) <= k + 1])
        while n < len(units) and (n < due or (reduced < rate * time and n < done[c] + LIMIT)):
            time, reduced, n = time + pe_unit(n), reduced + dve_unit(n), n + 1
        over = max(-CARRY, min(CARRY, reduced - rate * time))
        plan.append((list(range(a, n)), [x for x in range(len(done)) if a < done[x] <= n]))
    assert n == len(units)
    first_rows = [c for c in range(len(done)) if done[c] <= first]
    ends = [k for k in range(len(steps)) if k + 1 == len(steps) or steps[k + 1][1] == 0]

    ph = ExitStack()
    with ph:
        pt = [sb(f"pt{n}", [P, HPG, CH], f32, ph) for n in range(NP)]
        mxp = [sb(f"mxp{n}", [P, NC, TPC * HPG], f32, ph) for n in range(2)]
        mrow = [sb(f"mrow{n}", [P, TPC * HPG, 2], f16, ph) for n in range(2)]
        mcol = [sb(f"mcol{n}", [P, TPC * HPG], f32, ph) for n in range(2)]
        mt = [sb(f"mt{n}", [2 * HPG, CH], f16, ph) for n in range(2)]
        ot = sb("ot", [P, CH], f32, ph)
        rec = sb("rec", [P, TPC, HPG], f32, ph)
        mx = [pb(f"mx{n}", [P, CH], f32, ph) for n in range(NMX)]
        sc = [pb(f"sc{n}", [P, CH], f32, ph) for n in range(NSC)]
        pv = pb("pv", [P, CH], f32, ph)
        misc = pb("misc", [P, 1024], f16, ph)
        misc32 = misc[:, :].bitcast(f32)
        (s_mx, s_red, s_comb, s_mhi, s_mrow, s_mt, s_mte, s_m0, s_m1, s_sc, s_ex, s_msk, s_pv, s_oe, s_otr, s_on, s_rec) = S = sems(
            ph, "a_mx", "a_red", "a_comb", "a_mhi", "a_mrow", "a_mt", "a_mte", "a_m0", "a_m1", "a_sc", "a_ex", "a_msk", "a_pv",
            "a_oe", "a_otr", "a_on", "a_rec")
        s_m = [s_m0, s_m1]
        at = attn[:, :].rearrange("p (i c) -> p i c", c=D)

        def qcol(c, h):
            return (QGR[c] * 2 + h // 2) * T + QCH[c] * CH

        def kcol(c, h):
            return (QGR[c] * 2 + h % 2) * T

        def first_query(k):
            c, j = steps[k]
            return max(0, j - TPC * QCH[c]) * P

        def diagonals(k):
            return sum(j >= TPC * QCH[c] for c, j in steps[:k + 1])

        ph2 = ExitStack()
        with ph2:
            block = ph2.enter_context(nc.Block())

            @block.sync
            def _(sp):
                for c in range(len(done)):
                    sp.wait_ge(s_mte, c + 1)
                    for q in range(2):
                        to = qcol(c, 2 * q)
                        sp.dma_start(qs[M_ROW:M_ROW + 4, to:to + CH], mt[c % 2][4 * q:4 * q + 4, :]).then_inc(s_m[c % 2], 16)
                for n in range(2):
                    sp.wait_ge(s_m[n], 16 * len(done))

            @block.tensor
            def _(pe):
                n_rows, n_out = 0, 0

                def maximum(n):
                    c, tt, h, _n, c0, w, last = units[n]
                    if n >= NMX:
                        pe.wait_ge(s_red, n - NMX + 1)
                    out = mx[n % NMX]
                    mm = nc.tensor.matmul(out[:, 0:w], qs[:, qcol(c, h) + tt * P:qcol(c, h) + (tt + 1) * P],
                                          ks[:, kcol(c, h) + c0:kcol(c, h) + c0 + w], start=True, stop=not last)
                    if last:
                        mm = nc.tensor.matmul(out[:, w - P:w], idb[:, :], fut[:, :], start=False, stop=True)
                    mm.then_inc(s_mx, 1)

                def misc_free():
                    if n_rows:
                        pe.wait_ge(s_mte, n_rows)
                    if n_out:
                        pe.wait_ge(s_on, n_out)

                def maximum_rows(c):
                    pe.wait_ge(s_mrow, c + 1)
                    misc_free()
                    for tt in range(TPC):
                        mm = nc.tensor.transpose(misc[0:2 * HPG, tt * P:(tt + 1) * P],
                                                 mrow[c % 2][:, tt * HPG:(tt + 1) * HPG, :].rearrange("p a b -> p (a b)"), id16[:, :])
                    mm.then_inc(s_mt, 1)

                def scores(k, h):
                    c, j = steps[k]
                    r = first_query(k)
                    u = HPG * k + h
                    if u >= NSC:
                        pe.wait_ge(s_ex, u - NSC + 1)
                    nc.tensor.matmul(sc[u % NSC][:, 0:CH - r], ks[:, kcol(c, h) + j * P:kcol(c, h) + (j + 1) * P],
                                     qs[:, qcol(c, h) + r:qcol(c, h) + CH], start=True, stop=True).then_inc(s_sc, 1)

                def values(k):
                    c, j = steps[k]
                    r = first_query(k)
                    if j >= TPC * QCH[c]:
                        pe.wait_ge(s_msk, diagonals(k))
                    else:
                        pe.wait_ge(s_ex, HPG * (k + 1))
                    if j == 0:
                        if c:
                            pe.wait_ge(s_oe, c)
                    for h in range(HPG):
                        mm = nc.tensor.matmul(pv[32 * h:32 * h + 32, r:CH], vs[:, QGR[c], j, :], pt[k % NP][:, h, r:CH],
                                              start=(j == 0), stop=(k in ends), tile_position=(0, 32 * h))
                    mm.then_inc(s_pv, 1)

                def outputs(c):
                    pe.wait_ge(s_oe, c + 1)
                    misc_free()
                    for tt in range(TPC):
                        mm = nc.tensor.transpose(misc32[:, tt * P:(tt + 1) * P], ot[:, tt * P:(tt + 1) * P], id32[:, :])
                    mm.then_inc(s_otr, 1)

                for n in range(first):
                    maximum(n)
                for c in first_rows:
                    maximum_rows(c)
                    n_rows += 1
                rows = []
                for k, (c, j) in enumerate(steps):
                    us = list(plan[k][0])
                    if j == 0:
                        pe.wait_ge(s_m[c % 2], 32 * (c // 2 + 1))
                    for op, share in ORDER:
                        if op is not None:
                            scores(k, op)
                        elif k >= SKEW:
                            values(k - SKEW)
                        while us and (plan[k][0][-1] - len(us) + 1.5 - plan[k][0][0]) / len(plan[k][0]) <= share:
                            maximum(us.pop(0))
                    for x in rows:
                        maximum_rows(x)
                        n_rows += 1
                    rows = plan[k][1]
                    if j == SKEW and c:
                        outputs(c - 1)
                        n_out += 1
                for k in range(len(steps) - SKEW, len(steps)):
                    values(k)
                outputs(len(done) - 1)

            @block.scalar
            def _(act):
                def rows_out(c):
                    act.wait_ge(s_mt, c + 1)
                    if c >= 2:
                        act.wait_ge(s_m[c % 2], 32 * (c // 2))
                    nc.scalar.activation(mt[c % 2][:, :], misc[0:2 * HPG, 0:CH], ACT.Copy).then_inc(s_mte, 1)

                def output_out(c):
                    act.wait_ge(s_pv, ends[c] + 1)
                    if c:
                        act.wait_ge(s_otr, c)
                    nc.scalar.activation(ot[:, :], pv[:, :], ACT.Copy).then_inc(s_oe, 1)

                for c in first_rows:
                    rows_out(c)
                rows = []
                for k, (c, j) in enumerate(steps):
                    r = first_query(k)
                    if k >= NP:
                        act.wait_ge(s_pv, k - NP + 1)
                    for h in range(HPG):
                        u = HPG * k + h
                        act.wait_ge(s_sc, u + 1)
                        nc.scalar.activation(pt[k % NP][:, h, r:CH], sc[u % NSC][:, 0:CH - r], ACT.Exp,
                                             scale=DH ** -0.5).then_inc(s_ex, 1)
                        if h == 1 and j == SKEW - 1 and c:
                            output_out(c - 1)
                    for x in rows:
                        rows_out(x)
                    rows = plan[k][1]
                output_out(len(done) - 1)

            @block.gpsimd
            def _(pool):
                for k, (c, j) in enumerate(steps):
                    if j >= TPC * QCH[c]:
                        r = first_query(k)
                        pool.wait_ge(s_ex, HPG * (k + 1))
                        dg = pt[k % NP][:, :, r:r + P]
                        nc.gpsimd.affine_select(out=dg, in_=dg, compare_op=ALU.is_ge, fill=0.0, base=0,
                                                pattern=[[0, HPG], [1, P]], channel_multiplier=-1).then_inc(s_msk, 1)

            @block.vector
            def _(dve):
                def reduce(n):
                    c, tt, h, piece, _c0, w, _last = units[n]
                    dve.wait_ge(s_mx, n + 1)
                    if c >= 2:
                        dve.wait_ge(s_mrow, c - 1)
                    col = tt * HPG + h
                    nc.vector.reduce_max(mxp[c % 2][:, piece, col:col + 1], mx[n % NMX][:, 0:w], AX.X).then_inc(s_red, 1)

                def rows(c):
                    dve.wait_ge(s_red, done[c])
                    if c >= 2:
                        dve.wait_ge(s_mrow, c - 1)
                        dve.wait_ge(s_mt, c - 1)
                    m = mcol[c % 2]
                    nc.vector.reduce_max(m[:, :], mxp[c % 2][:, 0:QCH[c] + 1, :].rearrange("p n c -> p c n"), AX.X).then_inc(s_comb, 1)
                    dve.wait_ge(s_comb, c + 1)
                    nc.vector.tensor_scalar(mrow[c % 2][:, :, 0], m[:, :], -1.0 / M_ONE, None, ALU.mult).then_inc(s_mhi, 1)
                    dve.wait_ge(s_mhi, c + 1)
                    nc.vector.scalar_tensor_tensor(out=mrow[c % 2][:, :, 1], in0=m[:, :], scalar=-1.0 / M_ONE, in1=mrow[c % 2][:, :, 0],
                                                   op0=ALU.mult, op1=ALU.subtract).then_inc(s_mrow, 1)

                def divide(c):
                    g, J = QGR[c], QCH[c]
                    dve.wait_ge(s_otr, c + 1)
                    if c:
                        dve.wait_ge(s_on, c)
                    o = misc32.rearrange("p (t h c) -> p t h c", h=HPG, c=32)
                    nc.vector.reciprocal(rec[:, :, :], o[:, :, :, DH]).then_inc(s_rec, 1)
                    dve.wait_ge(s_rec, c + 1)
                    dst = at[:, J * TPC:(J + 1) * TPC, g * HPG * DH:(g + 1) * HPG * DH].rearrange("p t (h d) -> p t h d", d=DH)
                    nc.vector.tensor_tensor(dst, o[:, :, :, 0:DH],
                                            rec[:, :, :].rearrange("p t (h o) -> p t h o", o=1).to_broadcast([P, TPC, HPG, DH]),
                                            ALU.mult).then_inc(s_on, 1)

                for n in range(first):
                    reduce(n)
                for c in first_rows:
                    rows(c)
                for k, (c, j) in enumerate(steps):
                    for n in plan[k][0]:
                        reduce(n)
                    for x in plan[k][1]:
                        rows(x)
                    if j == SKEW and c:
                        divide(c - 1)
                divide(len(done) - 1)
        retire(S)


def route(nc, sb, pb, sems, retire, b, x, select, sel_w, attn, wo_w, b_o, gate_w, id32, x1, x1t, score):
    f32, f16 = mybir.dt.float32, mybir.dt.float16
    ACT = mybir.ActivationFunctionType
    ph = ExitStack()
    with ph:
        xin = sb("xin", [P, NT, D], f32, ph)
        ah = [sb(f"ah{n}", [P, D], f16, ph) for n in range(3)]
        al = [sb(f"al{n}", [P, D], f16, ph) for n in range(3)]
        st = sb("st", [P, NT, 6], f32, ph)
        mv = sb("mv", [P, NT, 2], f32, ph)
        eps = sb("eps", [P, 1], f32, ph)
        sd = sb("sd", [P, NT], f32, ph)
        rstd = sb("rstd", [P, NT], f32, ph)
        ap_ = [pb(f"ap{n}", [P, CH], f32, ph) for n in range(2)]
        wp_ = [pb(f"wp{n}", [P, CH], f32, ph) for n in range(2)]
        xp_ = [pb(f"xp{n}", [P, CH], f32, ph) for n in range(2)]
        lg = pb("lg", [P, CH], f32, ph)
        (s_x0, s_x1, s_x2, s_x3, s_xb, s_at, s_ah, s_al, s_w, s_y1, s_st, s_mv, s_sd, s_eps, s_rs, s_n, s_xt, s_xh, s_xl, s_lg, s_sig, s_sel) = S = sems(
            ph, "r_x0", "r_x1", "r_x2", "r_x3", "r_xb", "r_at", "r_ah", "r_al", "r_w", "r_y1", "r_st", "r_mv", "r_sd", "r_epsd", "r_rs", "r_n", "r_xt", "r_xh",
            "r_xl", "r_lg", "r_sig", "r_sel")
        s_x = [s_x0, s_x1, s_x2, s_x3]
        x1v = x1[:, :].rearrange("p (i c) -> p i c", c=D)

        ph2 = ExitStack()
        with ph2:
            block = ph2.enter_context(nc.Block())

            @block.sync
            def _(sp):
                for n in range(NC):
                    sp.dma_start(xin[:, n * TPC:(n + 1) * TPC, :],
                                 x[bass.ds(b, 1), n * CH:(n + 1) * CH, :].rearrange("o (i p) c -> p (o i) c", p=P)).then_inc(s_x[n], 16)
                sp.dma_start(sel_w[:, :, :], select).then_inc(s_sel, 16)
                sp.wait_ge(s_sel, 16)

            @block.gpsimd
            def _(pool):
                nc.gpsimd.memset(eps[:, :], EPS).then_inc(s_eps, 1)
                for i in range(NT):
                    if i % TPC == 0:
                        pool.wait_ge(s_x[i // TPC], 16)
                    nc.gpsimd.tensor_tensor(x1v[:, i, :], xin[:, i, :], b_o[:, :], ALU.add).then_inc(s_xb, 1)

            @block.tensor
            def _(pe):
                for s in range(NT + 8):
                    if s < NT:
                        i = s
                        if i >= 2:
                            pe.wait_ge(s_al, i - 1)
                        for c in range(C):
                            mm = nc.tensor.transpose(ap_[i % 2][:, c * P:(c + 1) * P], attn[:, i * D + c * P:i * D + (c + 1) * P], id32[:, :])
                        mm.then_inc(s_at, 1)
                    if 2 <= s < NT + 2:
                        i = s - 2
                        pe.wait_ge(s_al, i + 1)
                        if i >= 2:
                            pe.wait_ge(s_y1, i - 1)
                        n = 0
                        for c in range(C):
                            for part, wh in ((ah, 0), (ah, 1), (al, 0)):
                                mm = nc.tensor.matmul(wp_[i % 2][:, 0:D], part[i % 3][:, c * P:(c + 1) * P], wo_w[:, c, wh * D:(wh + 1) * D],
                                                      start=(n == 0), stop=(n == 3 * C - 1))
                                n += 1
                        mm.then_inc(s_w, 1)
                    if 6 <= s < NT + 6:
                        i = s - 6
                        pe.wait_ge(s_n, i + 1)
                        if i >= 2:
                            pe.wait_ge(s_xl, i - 1)
                        for c in range(C):
                            mm = nc.tensor.transpose(xp_[i % 2][:, c * P:(c + 1) * P], x1[:, i * D + c * P:i * D + (c + 1) * P], id32[:, :])
                        mm.then_inc(s_xt, 1)
                    if s >= 8:
                        i = s - 8
                        pe.wait_ge(s_xl, i + 1)
                        n = 0
                        for c in range(C):
                            for xh, wh in ((0, 0), (0, 1), (1, 0)):
                                mm = nc.tensor.matmul(lg[:, i * NE:(i + 1) * NE], x1t[:, xh, c, i * P:(i + 1) * P], gate_w[:, c, wh, :],
                                                      start=(n == 0), stop=(n == 3 * C - 1))
                                n += 1
                        mm.then_inc(s_lg, 1)

            @block.scalar
            def _(act):
                act.wait_ge(s_eps, 1)
                for s in range(NT + 6):
                    if s < NT:
                        i = s
                        act.wait_ge(s_at, i + 1)
                        if i >= 3:
                            act.wait_ge(s_w, i - 2)
                        nc.scalar.activation(ah[i % 3][:, :], ap_[i % 2][:, 0:D], ACT.Copy).then_inc(s_ah, 1)
                    if 4 <= s < NT + 4:
                        i = s - 4
                        act.wait_ge(s_mv, i + 1)
                        nc.scalar.activation(sd[:, i:i + 1], mv[:, i, 1:2], ACT.Sqrt, bias=eps[:, :]).then_inc(s_sd, 1)
                    if s >= 6:
                        i = s - 6
                        act.wait_ge(s_xt, i + 1)
                        nc.scalar.activation(x1t[:, 0, :, i * P:(i + 1) * P], xp_[i % 2][:, 0:D].rearrange("p (c t) -> p c t", c=C),
                                             ACT.Copy).then_inc(s_xh, 1)
                act.wait_ge(s_lg, NT)
                nc.scalar.activation(score[:, :, :], lg[:, :].rearrange("p (i e) -> p i e", e=NE), ACT.Sigmoid,
                                     scale=1.0 / W_GATE).then_inc(s_sig, 1)

            @block.vector
            def _(dve):
                for s in range(NT + 7):
                    if 5 <= s < NT + 5:
                        i = s - 5
                        dve.wait_ge(s_sd, i + 1)
                        nc.vector.reciprocal(rstd[:, i:i + 1], sd[:, i:i + 1]).then_inc(s_rs, 1)
                    if 1 <= s <= NT:
                        i = s - 1
                        dve.wait_ge(s_ah, i + 1)
                        if i >= 3:
                            dve.wait_ge(s_w, i - 2)
                        nc.vector.tensor_tensor(al[i % 3][:, :], ap_[i % 2][:, 0:D], ah[i % 3][:, :], ALU.subtract).then_inc(s_al, 1)
                    if 5 <= s < NT + 5:
                        i = s - 5
                        dve.wait_ge(s_rs, i + 1)
                        nc.vector.tensor_scalar(x1v[:, i, :], x1v[:, i, :], mv[:, i, 0:1], rstd[:, i:i + 1],
                                                ALU.subtract, ALU.mult).then_inc(s_n, 1)
                    if 3 <= s < NT + 3:
                        i = s - 3
                        dve.wait_ge(s_w, i + 1)
                        dve.wait_ge(s_xb, i + 1)
                        nc.vector.tensor_tensor(x1v[:, i, :], wp_[i % 2][:, 0:D], x1v[:, i, :], ALU.add).then_inc(s_y1, 1)
                    if s >= 7:
                        i = s - 7
                        dve.wait_ge(s_xh, i + 1)
                        nc.vector.tensor_tensor(x1t[:, 1, :, i * P:(i + 1) * P], xp_[i % 2][:, 0:D].rearrange("p (c t) -> p c t", c=C),
                                                x1t[:, 0, :, i * P:(i + 1) * P], ALU.subtract).then_inc(s_xl, 1)
                    if 3 <= s < NT + 3:
                        i = s - 3
                        dve.wait_ge(s_y1, i + 1)
                        nc.vector.bn_stats(st[:, i, :], x1v[:, i, :]).then_inc(s_st, 1)
                        dve.wait_ge(s_st, i + 1)
                        nc.vector.bn_aggr(mv[:, i, :], st[:, i, :]).then_inc(s_mv, 1)
        retire(S)


def experts(nc, sb, pb, sems, retire, b, up_w, dn_w, sel_w, b_e, id16, x1, x1t, score, ct, out):
    f32, f16 = mybir.dt.float32, mybir.dt.float16
    ACT = mybir.ActivationFunctionType
    NB, SKEW = 4, 2
    STEPS = NC * NX
    AX = mybir.AxisListType
    EARLY = NX - NE
    ROUTE = 16
    ph = ExitStack()
    with ph:
        bsc = sb("bsc", [P, TPC, NE], f32, ph)
        pmax = sb("pmax", [P, TPC, NGR, 2], f32, ph)
        psum2 = sb("psum2", [P, TPC, NGR, 2], f32, ph)
        gsc = sb("gsc", [P, TPC, NGR], f32, ph)
        gs2 = sb("gs2", [P, TPC, NGR], f32, ph)
        gtop = sb("gtop", [P, TPC, 8], f32, ph)
        grep = sb("grep", [P, TPC, NGR], f32, ph)
        gsel = sb("gsel", [P, TPC, NGR], f32, ph)
        masked = sb("masked", [P, TPC, NE], f32, ph)
        etop = sb("etop", [P, TPC, 8], f32, ph)
        erep = sb("erep", [P, TPC, NE], f32, ph)
        wgt = sb("wgt", [P, TPC, NE], f32, ph)
        wsum = sb("wsum", [P, TPC], f32, ph)
        cst = sb("cst", [P, TPC, P], f16, ph)
        r = [sb(f"e_r{k}", [P, CH], f32, ph) for k in range(NB)]
        r2 = [sb(f"e_r2{k}", [P, CH], f32, ph) for k in range(NB)]
        h = [sb(f"e_h{k}", [P, CH], f32, ph) for k in range(NB)]
        hh = [sb(f"e_hh{k}", [P, CH], f16, ph) for k in range(NB)]
        hl = [sb(f"e_hl{k}", [P, CH], f16, ph) for k in range(NB)]
        st = sb("e_st", [P, TPC, 6], f32, ph)
        mv = sb("e_mv", [P, TPC, 2], f32, ph)
        eps = sb("e_eps", [P, 1], f32, ph)
        sd = sb("e_sd", [P, TPC], f32, ph)
        rstd = sb("e_rstd", [P, TPC], f32, ph)
        yo = [sb(f"e_yo{k}", [P, TPC, D], f32, ph) for k in range(2)]
        z = [pb(f"e_z{k}", [P, CH], f32, ph) for k in range(2)]
        cb = [pb(f"e_cb{k}", [P, CH], f32, ph) for k in range(2)]
        o = [[pb(f"e_o{n}{k}", [P, 2 * D], f32, ph) for k in range(2)] for n in range(2)]
        (s_z, s_r, s_r2, s_cb, s_h, s_hi, s_lo, s_dn, s_t2, s_st, s_mv, s_sd, s_eps, s_rs, s_n, s_rt, s_c0, s_ct, s_ctt, s_cte, s_out0, s_out1) = S = sems(
            ph, "e_z", "e_r", "e_r2", "e_cb", "e_h", "e_hi", "e_lo", "e_dn", "e_t2", "e_st", "e_mv", "e_sd", "e_epsd", "e_rs",
            "e_n", "e_route", "e_c0", "e_ct", "e_ctt", "e_cte", "e_out0", "e_out1")
        s_out = [s_out0, s_out1]
        un = 1.0 / (H_SCALE * W_DN)
        x1v = x1[:, :].rearrange("p (i c) -> p i c", c=D)
        outv = out.rearrange("b (i p) c -> p (b i) c", p=P)

        def expert(s):
            return (s - EARLY) % NX if s % NX >= EARLY else NE + s % NX

        def has_weight(s):
            return s % NX >= EARLY

        def weighted(s):
            return s // NX * NE + max(0, s % NX - EARLY)

        def selection(s):
            if s < 3:
                return 0, s
            n, at = s // NX + 1, s % NX - ROUTE
            return (n, at) if n < NC and 0 <= at < 3 else None

        def stage(s, n):
            c, e = divmod(s - SKEW - n, NX)
            return c - 1 if e == 0 and 1 <= c <= NC else None

        ph2 = ExitStack()
        with ph2:
            block = ph2.enter_context(nc.Block())

            @block.tensor
            def _(pe):
                for s in range(STEPS + SKEW):
                    if s < STEPS:
                        n, e, w = s // NX, expert(s), weighted(s)
                        if s >= 2:
                            pe.wait_ge(s_r, s - 1)
                        k = 0
                        for c in range(C):
                            for xh, wh in ((0, 0), (1, 0), (0, 1)):
                                mm = nc.tensor.matmul(z[s % 2][:, :], up_w[:, e, c, wh, :], x1t[:, xh, c, n * CH:(n + 1) * CH],
                                                      start=(k == 0), stop=(k == 3 * C - 1))
                                k += 1
                        mm.then_inc(s_z, 1)
                        if has_weight(s):
                            if s % NX == EARLY:
                                pe.wait_ge(s_cte, n + 1)
                            if w >= 2:
                                pe.wait_ge(s_h, w - 1)
                            nc.tensor.matmul(cb[w % 2][:, :], sel_w[:, e, :], ct[:, n * CH:(n + 1) * CH],
                                             start=True, stop=True).then_inc(s_cb, 1)
                    if s >= SKEW:
                        d = s - SKEW
                        n, e, at_first, at_last = d // NX, expert(d), d % NX == 0, d % NX == NX - 1
                        pe.wait_ge(s_lo, d + 1)
                        if at_first and n >= 2:
                            pe.wait_ge(s_t2, 2 * (n - 1))
                        for k in range(TPC):
                            bank, at = o[n % 2][k // 2], k % 2 * D
                            for q, (part, wh) in enumerate(((hh, 0), (hh, 1), (hl, 0))):
                                mm = nc.tensor.matmul(bank[:, at:at + D], part[d % NB][:, k * P:(k + 1) * P], dn_w[:, e, wh * D:(wh + 1) * D],
                                                      start=(at_first and k % 2 == 0 and q == 0), stop=(at_last and k % 2 == 1 and q == 2))
                        mm.then_inc(s_dn, 1)
                    if s < STEPS and s % NX == EARLY - 1:
                        n, w = s // NX, weighted(s)
                        pe.wait_ge(s_ct, 2 * (n + 1))
                        if w:
                            pe.wait_ge(s_h, w)
                        for k in range(TPC):
                            mm = nc.tensor.transpose(cb[1][:, :].bitcast(f16)[:, k * P:(k + 1) * P], cst[:, k, :], id16[:, :])
                        mm.then_inc(s_ctt, 1)

            @block.scalar
            def _(act):
                act.wait_ge(s_eps, 1)
                for s in range(STEPS + SKEW + 4):
                    if s < STEPS and s % NX == EARLY:
                        n = s // NX
                        act.wait_ge(s_ctt, n + 1)
                        nc.scalar.activation(ct[:, n * CH:(n + 1) * CH], cb[1][:, :].bitcast(f16)[:, 0:CH], ACT.Copy).then_inc(s_cte, 1)
                    if s < STEPS:
                        act.wait_ge(s_z, s + 1)
                        if s >= NB:
                            act.wait_ge(s_r2, s - NB + 1)
                        nc.scalar.activation(r[s % NB][:, :], z[s % 2][:, :], ACT.Relu, scale=H_SCALE ** 0.5 / W_UP).then_inc(s_r, 1)
                    if 1 <= s <= STEPS:
                        d = s - 1
                        if has_weight(d):
                            act.wait_ge(s_h, weighted(d) + 1)
                            src = h
                        else:
                            act.wait_ge(s_r2, d + 1)
                            src = r2
                        if d >= NB:
                            act.wait_ge(s_dn, d - NB + 1)
                        nc.scalar.activation(hh[d % NB][:, :], src[d % NB][:, :], ACT.Copy).then_inc(s_hi, 1)
                    n = stage(s, 3)
                    if n is not None:
                        act.wait_ge(s_mv, TPC * (n + 1))
                        if n:
                            act.wait_ge(s_rs, n)
                        nc.scalar.activation(sd[:, :], mv[:, :, 1], ACT.Sqrt, bias=eps[:, :]).then_inc(s_sd, 1)

            @block.gpsimd
            def _(pool):
                nc.gpsimd.memset(cst[:, :, :], 0.0).then_inc(s_c0, 1)
                nc.gpsimd.memset(eps[:, :], EPS).then_inc(s_eps, 1)
                for s in range(STEPS):
                    pool.wait_ge(s_r, s + 1)
                    if s >= NB:
                        pool.wait_ge(s_lo, s - NB + 1)
                    nc.gpsimd.tensor_tensor(r2[s % NB][:, :], r[s % NB][:, :], r[s % NB][:, :], ALU.mult).then_inc(s_r2, 1)

            @block.vector
            def _(dve):
                linked = [0]
                V = nc.vector

                def link(*ops):
                    for op in ops:
                        op.then_inc(s_rt, 1)
                    linked[0] += len(ops)
                    dve.wait_ge(s_rt, linked[0])

                def select_groups(n):
                    sc4 = score[:, n * TPC:(n + 1) * TPC, :]
                    link(V.tensor_tensor(bsc[:, :, :], sc4, b_e[:, :].rearrange("p (o e) -> p o e", o=1).to_broadcast([P, TPC, NE]), ALU.add))
                    pr = bsc[:, :, :].rearrange("p i (g a e) -> p (i g) a e", a=2, e=2)
                    pm, p2 = (t[:, :, :, :].rearrange("p i g a -> p (i g) a") for t in (pmax, psum2))
                    link(V.tensor_tensor(pm, pr[:, :, :, 0], pr[:, :, :, 1], ALU.max), V.tensor_tensor(p2, pr[:, :, :, 0], pr[:, :, :, 1], ALU.add))
                    gv, g2 = (t[:, :, :].rearrange("p i g -> p (i g)") for t in (gsc, gs2))
                    link(V.tensor_tensor(gv, pm[:, :, 0], pm[:, :, 1], ALU.add), V.tensor_tensor(g2, p2[:, :, 0], p2[:, :, 1], ALU.max))
                    link(V.tensor_tensor(gv, gv, g2, ALU.max))
                    link(*[V.max(gtop[:, i, :], gsc[:, i, :]) for i in range(TPC)])
                    link(V.memset(gtop[:, :, TOPG:8], BIG))
                    link(*[V.match_replace(grep[:, i, :], gtop[:, i, :], gsc[:, i, :], -BIG) for i in range(TPC)])

                def select_experts(n):
                    sc4 = score[:, n * TPC:(n + 1) * TPC, :]
                    link(V.tensor_scalar(gsel[:, :, :], grep[:, :, :], -BIG, None, ALU.is_equal))
                    link(V.tensor_tensor(masked[:, :, :].rearrange("p i (g e) -> p (i g) e", e=EPG), bsc[:, :, :].rearrange("p i (g e) -> p (i g) e", e=EPG),
                                         gsel[:, :, :].rearrange("p i (g o) -> p (i g) o", o=1).to_broadcast([P, TPC * NGR, EPG]), ALU.mult))
                    link(*[V.max(etop[:, i, :], masked[:, i, :]) for i in range(TPC)])
                    link(V.memset(etop[:, :, TOPK:8], BIG))
                    link(*[V.match_replace(erep[:, i, :], etop[:, i, :], masked[:, i, :], -BIG) for i in range(TPC)])
                    link(V.scalar_tensor_tensor(out=wgt[:, :, :], in0=erep[:, :, :], scalar=-BIG, in1=sc4, op0=ALU.is_equal, op1=ALU.mult))

                def normalise(n):
                    link(V.reduce_sum(wsum[:, :], wgt[:, :, :], AX.X))
                    link(V.tensor_scalar(wsum[:, :], wsum[:, :], 1e-20, None, ALU.add))
                    link(V.reciprocal(wsum[:, :], wsum[:, :]))
                    link(V.scalar_tensor_tensor(out=wgt[:, :, :], in0=wgt[:, :, :], scalar=2.5,
                                                in1=wsum[:, :].rearrange("p (i o) -> p i o", o=1).to_broadcast([P, TPC, NE]), op0=ALU.mult, op1=ALU.mult))
                    if n == 0:
                        dve.wait_ge(s_c0, 1)
                    else:
                        dve.wait_ge(s_ctt, n)
                    V.tensor_copy(cst[:, :, 0:NE], wgt[:, :, :]).then_inc(s_ct, 1)
                    dve.wait_ge(s_ct, 2 * n + 1)
                    V.tensor_tensor(cst[:, :, NX:NX + NE], wgt[:, :, :], cst[:, :, 0:NE], ALU.subtract).then_inc(s_ct, 1)

                for s in range(STEPS + SKEW + 6):
                    if 1 <= s <= STEPS:
                        d = s - 1
                        dve.wait_ge(s_hi, d + 1)
                        if d >= NB:
                            dve.wait_ge(s_dn, d - NB + 1)
                        src = h if has_weight(d) else r2
                        nc.vector.tensor_tensor(hl[d % NB][:, :], src[d % NB][:, :], hh[d % NB][:, :], ALU.subtract).then_inc(s_lo, 1)
                    if s < STEPS and has_weight(s):
                        w = weighted(s)
                        dve.wait_ge(s_r2, s + 1)
                        dve.wait_ge(s_cb, w + 1)
                        if s >= NB:
                            dve.wait_ge(s_lo, s - NB + 1)
                        nc.vector.tensor_tensor(h[s % NB][:, :], r2[s % NB][:, :], cb[w % 2][:, :], ALU.mult).then_inc(s_h, 1)
                    part = selection(s)
                    if part is not None:
                        (select_groups, select_experts, normalise)[part[1]](part[0])
                    n = stage(s, 0)
                    if n is not None:
                        dve.wait_ge(s_dn, (n + 1) * NX)
                        for q in range(2):
                            xr = x1[:, (n * TPC + 2 * q) * D:(n * TPC + 2 * q + 2) * D]
                            nc.vector.scalar_tensor_tensor(out=xr, in0=o[n % 2][q][:, :], scalar=un, in1=xr,
                                                           op0=ALU.mult, op1=ALU.add).then_inc(s_t2, 1)
                    n = stage(s, 2)
                    if n is not None:
                        dve.wait_ge(s_t2, 2 * (n + 1))
                        for k in range(TPC):
                            nc.vector.bn_stats(st[:, k, :], x1v[:, n * TPC + k, :]).then_inc(s_st, 1)
                        for k in range(TPC):
                            dve.wait_ge(s_st, TPC * n + k + 1)
                            nc.vector.bn_aggr(mv[:, k, :], st[:, k, :]).then_inc(s_mv, 1)
                    n = stage(s, 4)
                    if n is not None:
                        dve.wait_ge(s_sd, n + 1)
                        nc.vector.reciprocal(rstd[:, :], sd[:, :]).then_inc(s_rs, 1)
                        dve.wait_ge(s_rs, n + 1)
                        if n >= 2:
                            dve.wait_ge(s_out[n % 2], 16 * (n // 2))
                        for k in range(TPC):
                            nc.vector.tensor_scalar(yo[n % 2][:, k, :], x1v[:, n * TPC + k, :], mv[:, k, 0:1], rstd[:, k:k + 1],
                                                    ALU.subtract, ALU.mult).then_inc(s_n, 1)

            @block.sync
            def _(sp):
                for n in range(NC):
                    sp.wait_ge(s_n, TPC * (n + 1))
                    sp.dma_start(outv[:, bass.ds(b * NT + n * TPC, TPC), :], yo[n % 2][:, :, :]).then_inc(s_out[n % 2], 16)
                for k in range(2):
                    sp.wait_ge(s_out[k], 16 * (NC // 2))
        retire(S)


def kernel(**inputs):
    import ml_dtypes
    import concourse.bacc as _bacc
    from concourse.bass_utils import run_bass_kernel_spmd as _run

    a = {k.removeprefix("L0_"): np.asarray(v) for k, v in inputs.items()}

    def rows(w):
        return w.reshape(C, P, -1).transpose(1, 0, 2)

    def every(v):
        return np.broadcast_to(v.reshape(1, -1), (P, v.size))

    up = np.concatenate([a["ffn_up_w"], a["ffn_shared_up_w"].reshape(NSH // FI, FI, D)])
    down = np.concatenate([a["ffn_down_w"], a["ffn_shared_down_w"].reshape(D, NSH // FI, FI).transpose(1, 0, 2)])
    arrays = {
        "x": a["attn_x"],
        "xt": a["attn_x"].reshape(B, T, C, P).transpose(0, 3, 2, 1),
        "wqkv": rows(np.concatenate([a["attn_Wq"], a["attn_Wk"], a["attn_Wv"]], axis=1)),
        "bqkv": every(np.concatenate([a["attn_bq"], a["attn_bk"], a["attn_bv"]])),
        "wo": rows(a["attn_Wo"]),
        "bo": every(a["attn_bo"]),
        "gate": rows(a["ffn_gate_w"].T),
        "ebias": every(a["ffn_e_bias"]),
        "up": up.reshape(NX, FI, C, P).transpose(3, 0, 2, 1),
        "down": down.transpose(2, 0, 1),
    }
    pos = np.arange(T, dtype=np.float32)[:, None]
    freq = np.exp(-(np.arange(0, DH, 2, dtype=np.float32) / DH) * np.log(np.float32(10000.0)))
    angle = pos * freq
    cos = np.repeat(np.cos(angle), 2, axis=1)
    sin = np.stack([-np.sin(angle), np.sin(angle)], axis=-1).reshape(T, DH)
    tiles = lambda t: t.reshape(NT, P, DH).transpose(1, 0, 2).astype(np.float32)
    select = np.zeros((P, NX, P), np.float16)
    for e in range(NX):
        select[e, e] = select[NX + e, e] = 1.0
    arrays |= {
        "rope_cos": tiles(cos), "rope_sin": tiles(sin),
        "eye32": np.eye(P, dtype=np.float32), "eye16": np.eye(P, dtype=np.float16), "eyeb": np.eye(P, dtype=ml_dtypes.bfloat16),
        "future": np.where(np.arange(P)[None, :] > np.arange(P)[:, None], -1e30, 0.0).astype(ml_dtypes.bfloat16),
        "select": select,
    }
    nc = _bacc.Bacc("TRN2", target_bir_lowering=False, num_devices=1)
    aps = {}
    for name, v in arrays.items():
        arrays[name] = v = np.ascontiguousarray(v)
        aps[name] = nc.dram_tensor(name, v.shape, mybir.dt.from_np(v.dtype), kind="ExternalInput").ap()
    aps["out"] = nc.dram_tensor("out", (B, T, D), mybir.dt.float32, kind="ExternalOutput").ap()
    nc.disable_value_cache = True
    layer(nc, **aps)
    return _run(nc, [arrays], core_ids=[0]).results[0]["out"]
```
